# Optimizing a Trainium2 kernel written in Bass

```python
import numpy as np
import jax
import jax.numpy as jnp

def _softmax(x, axis=-1):
    return jax.nn.softmax(x, axis=axis)

def _gelu(x):
    return jax.nn.gelu(x, approximate=True)

def _silu(x):
    return jax.nn.silu(x)

def _sigmoid(x):
    return jax.nn.sigmoid(x)

def _layernorm(x, axis=-1, eps=1e-05):
    m = jnp.mean(x, axis=axis, keepdims=True)
    v = jnp.var(x, axis=axis, keepdims=True)
    return (x - m) / jnp.sqrt(v + eps)

def _scatter_add(tgt, idx, src, axis=0):
    return tgt.at[idx].add(src)

def _segment_sum(src, seg, n):
    return jax.ops.segment_sum(src, seg, n)
kernel_name = 'mk_adaln_ffn_d2_seqx_r4_6dad5e'

def setup_inputs(seed: int=0):
    np.random.seed(seed)
    _w = jnp.asarray

    def _rec_inputs():
        import jax
        import jax.numpy as jnp
        _rk = jax.random.key(seed)
        x = -0.000125 + 0.9999 * jax.random.normal(jax.random.fold_in(_rk, 1), (8, 256, 1024), jnp.float32)
        _lenS = 256 - jax.random.randint(jax.random.fold_in(_rk, 7), (8,), 0, max(1, 256 // 4) + 1, jnp.int32)
        _lenS2 = 256 - jax.random.randint(jax.random.fold_in(_rk, 8), (8,), 0, max(1, 256 // 4) + 1, jnp.int32)
        itok_B_0_7 = jax.random.randint(jax.random.fold_in(_rk, 11), (8,), 0, 8, jnp.int32)
        itok_B_0_23 = jax.random.randint(jax.random.fold_in(_rk, 12), (8,), 0, 24, jnp.int32)
        return (x, itok_B_0_7, itok_B_0_23)
    x, itok_B_0_7, itok_B_0_23 = _rec_inputs()

    def _L0_cond_setup():
        import jax, jax.numpy as jnp
        import numpy as np
        TOP_K = 2
        LANG_BIAS = 5.0
        SCALING = 32.0 / 16.0
        LANGUAGE_PAD_ID = -1
        key = jax.random.key(seed)
        ks = jax.random.split(key, 6)
        B, T, D, O, E, R = (4, 512, 1024, 1024, 8, 16)
        x = jax.random.normal(ks[0], (B, T, D), dtype=jnp.float32)
        language_ids = jax.random.randint(ks[1], (B,), 0, E).astype(jnp.int64)
        W = jax.random.normal(ks[2], (O, D), dtype=jnp.float32) * (1.0 / np.sqrt(D))
        Wr = jax.random.normal(ks[3], (E, D), dtype=jnp.float32) * (1.0 / np.sqrt(D))
        A = jax.random.normal(ks[4], (E, R, D), dtype=jnp.float32) * (1.0 / np.sqrt(D))
        Bm = jax.random.normal(ks[5], (O, R), dtype=jnp.float32) * 0.0
        Bm = jnp.broadcast_to(Bm, (E, O, R)) + jax.random.normal(ks[5], (E, O, R), dtype=jnp.float32) * 0.02
        return {'x': x, 'language_ids': language_ids, 'W': W, 'Wr': Wr, 'A': A, 'B': Bm}
    _L0_cond_all = _L0_cond_setup()
    _L0_cond_in = {k: v for k, v in _L0_cond_all.items() if k in ('W', 'Wr', 'A', 'B')}
    del _L0_cond_all

    def _L0_ffn_setup():
        import jax, jax.numpy as jnp
        import numpy as np
        R = 16
        LORA_ALPHA = 16
        SCALING = LORA_ALPHA / R
        key = jax.random.key(seed)
        kx, kr, ka = jax.random.split(key, 3)
        B, S, D, DO, E = (4, 512, 1024, 1024, 8)
        x = jax.random.normal(kx, (B, S, D), dtype=jnp.float32)
        bound_r = 1.0 / np.sqrt(D)
        route_w = jax.random.uniform(kr, (E, D), jnp.float32, -bound_r, bound_r)
        bound_a = 1.0 / np.sqrt(D)
        A = jax.random.uniform(ka, (E, R, D), jnp.float32, -bound_a, bound_a)
        kb = jax.random.fold_in(key, 7)
        Bw = jax.random.normal(kb, (E, DO, R), dtype=jnp.float32) * 0.02
        return {'x': x, 'route_w': route_w, 'A': A, 'Bw': Bw}
    _L0_ffn_all = _L0_ffn_setup()
    _L0_ffn_in = {k: v for k, v in _L0_ffn_all.items() if k in ('route_w', 'A', 'Bw')}
    del _L0_ffn_all

    def _L1_cond_setup():
        import jax, jax.numpy as jnp
        import numpy as np
        R = 16
        ALPHA = 32
        SCALING = ALPHA / R
        SLOTS = 32
        IN_F = 1024
        OUT_F = 1024
        B, T = (8, 256)
        key = jax.random.key(seed)
        k1, k2, k3, k4, k5, k6 = jax.random.split(key, 6)
        x = jax.random.normal(k1, (B, T, IN_F), dtype=jnp.float32)
        adapter_mapping = jax.random.randint(k2, (B,), 0, SLOTS, dtype=jnp.int32)
        W = jax.random.normal(k3, (OUT_F, IN_F), dtype=jnp.float32) * 0.02
        b = jax.random.normal(k4, (OUT_F,), dtype=jnp.float32) * 0.02
        lora_As = jax.random.normal(k5, (SLOTS, IN_F, R), dtype=jnp.float32) * 0.02
        lora_Bs = jax.random.normal(k6, (SLOTS, R, OUT_F), dtype=jnp.float32) * 0.02
        return {'x': x, 'adapter_mapping': adapter_mapping, 'W': W, 'b': b, 'lora_As': lora_As, 'lora_Bs': lora_Bs}
    _L1_cond_all = _L1_cond_setup()
    _L1_cond_in = {k: v for k, v in _L1_cond_all.items() if k in ('W', 'b', 'lora_As', 'lora_Bs')}
    del _L1_cond_all

    def _L1_ffn_setup():
        import jax, jax.numpy as jnp
        import numpy as np
        NUM_EXPERTS = 8
        TOP_K = 2
        RANK = 16
        LORA_ALPHA = 32
        SCALING = LORA_ALPHA / RANK
        key = jax.random.key(seed)
        ks = jax.random.split(key, 6)
        B, S, D_IN, D_OUT = (4, 512, 1024, 1024)
        x = jax.random.normal(ks[0], (B, S, D_IN), dtype=jnp.float32)
        W_base = jax.random.normal(ks[1], (D_OUT, D_IN), dtype=jnp.float32) * 0.02
        b_base = jax.random.normal(ks[2], (D_OUT,), dtype=jnp.float32) * 0.02
        W_router = jax.random.normal(ks[3], (NUM_EXPERTS, D_IN), dtype=jnp.float32) * 0.02
        A = jax.random.normal(ks[4], (NUM_EXPERTS, RANK, D_IN), dtype=jnp.float32) * 0.02
        Bm = jax.random.normal(ks[5], (D_OUT, RANK), dtype=jnp.float32) * 0.02
        Bm = jnp.broadcast_to(Bm, (NUM_EXPERTS, D_OUT, RANK)) * jnp.arange(1, NUM_EXPERTS + 1, dtype=jnp.float32)[:, None, None] * 0.2
        return {'x': x, 'W_base': W_base, 'b_base': b_base, 'W_router': W_router, 'A': A, 'B': Bm}
    _L1_ffn_all = _L1_ffn_setup()
    _L1_ffn_in = {k: v for k, v in _L1_ffn_all.items() if k in ('W_base', 'b_base', 'W_router', 'A', 'B')}
    del _L1_ffn_all
    return {'x': x, 'itok_B_0_7': itok_B_0_7, 'itok_B_0_23': itok_B_0_23, 'L0_cond_W': _L0_cond_in['W'], 'L0_cond_Wr': _L0_cond_in['Wr'], 'L0_cond_A': _L0_cond_in['A'], 'L0_cond_B': _L0_cond_in['B'], 'L0_ffn_route_w': _L0_ffn_in['route_w'], 'L0_ffn_A': _L0_ffn_in['A'], 'L0_ffn_Bw': _L0_ffn_in['Bw'], 'L1_cond_W': _L1_cond_in['W'], 'L1_cond_b': _L1_cond_in['b'], 'L1_cond_lora_As': _L1_cond_in['lora_As'], 'L1_cond_lora_Bs': _L1_cond_in['lora_Bs'], 'L1_ffn_W_base': _L1_ffn_in['W_base'], 'L1_ffn_b_base': _L1_ffn_in['b_base'], 'L1_ffn_W_router': _L1_ffn_in['W_router'], 'L1_ffn_A': _L1_ffn_in['A'], 'L1_ffn_B': _L1_ffn_in['B']}

def reference(x, itok_B_0_7, itok_B_0_23, L0_cond_W, L0_cond_Wr, L0_cond_A, L0_cond_B, L0_ffn_route_w, L0_ffn_A, L0_ffn_Bw, L1_cond_W, L1_cond_b, L1_cond_lora_As, L1_cond_lora_Bs, L1_ffn_W_base, L1_ffn_b_base, L1_ffn_W_router, L1_ffn_A, L1_ffn_B):
    import jax
    import jax.numpy as jnp

    def _L0_cond_ref(x, language_ids, W, Wr, A, B):
        import jax, jax.numpy as jnp
        import numpy as np
        TOP_K = 2
        LANG_BIAS = 5.0
        SCALING = 32.0 / 16.0
        LANGUAGE_PAD_ID = -1
        base = jnp.einsum('btd,od->bto', x, W)
        E = Wr.shape[0]
        logits = jnp.einsum('btd,ed->bte', x.astype(jnp.float32), Wr.astype(jnp.float32))
        expert_targets = language_ids
        valid = expert_targets >= 0
        tgt = jnp.where(valid, expert_targets, 0)
        bias = jax.nn.one_hot(tgt, E, dtype=logits.dtype) * LANG_BIAS
        bias = jnp.where(valid[:, None], bias, 0.0)
        logits = logits + bias[:, None, :]
        topw, topi = jax.lax.top_k(logits, TOP_K)
        weights = jax.nn.softmax(topw, axis=-1)
        gates = jnp.sum(jax.nn.one_hot(topi, E, dtype=weights.dtype) * weights[..., None], axis=-2)
        gates = gates.astype(x.dtype)
        h = jnp.einsum('btd,erd->bter', x, A)
        lora_out = jnp.einsum('bter,bte,eor->bto', h, gates, B)
        return base + SCALING * lora_out

    def _L0_ffn_ref(x, route_w, A, Bw):
        import jax, jax.numpy as jnp
        import numpy as np
        R = 16
        LORA_ALPHA = 16
        SCALING = LORA_ALPHA / R
        logits = jnp.einsum('bsd,ed->bse', x, route_w)
        topk_v, topk_idx = jax.lax.top_k(logits, 1)
        E = logits.shape[-1]
        route_weight = jax.nn.one_hot(topk_idx[..., 0], E, dtype=logits.dtype) * topk_v
        h = jnp.einsum('bsd,erd->bser', x, A)
        wh = route_weight[..., None] * h
        out = jnp.einsum('bser,eor->bso', wh, Bw) * SCALING
        return out

    def _L1_cond_ref(x, adapter_mapping, W, b, lora_As, lora_Bs):
        import jax, jax.numpy as jnp
        import numpy as np
        R = 16
        ALPHA = 32
        SCALING = ALPHA / R
        SLOTS = 32
        IN_F = 1024
        OUT_F = 1024
        B, T = (8, 256)
        base_out = jnp.einsum('bti,oi->bto', x, W) + b
        A = lora_As[adapter_mapping]
        Bm = lora_Bs[adapter_mapping]
        lora_h = jnp.einsum('bti,bir->btr', x, A)
        lora_out = jnp.einsum('btr,bro->bto', lora_h, Bm)
        return base_out + lora_out * SCALING

    def _L1_ffn_ref(x, W_base, b_base, W_router, A, B):
        import jax, jax.numpy as jnp
        import numpy as np
        NUM_EXPERTS = 8
        TOP_K = 2
        RANK = 16
        LORA_ALPHA = 32
        SCALING = LORA_ALPHA / RANK
        bs, seq, d_in = x.shape
        T = bs * seq
        xf = x.reshape(T, d_in)
        base = xf @ W_base.T + b_base
        logits = xf @ W_router.T
        rw, sel = jax.lax.top_k(logits, TOP_K)
        rw = jax.nn.softmax(rw, axis=-1)
        onehot = jax.nn.one_hot(sel, NUM_EXPERTS, dtype=rw.dtype)
        w = jnp.einsum('tk,tke->te', rw, onehot)
        h = jnp.einsum('td,erd->ter', xf, A)
        lora = jnp.einsum('ter,te,eor->to', h, w, B) * SCALING
        return (base + lora).reshape(bs, seq, -1)
    x = x + _L0_ffn_ref(_L0_cond_ref(x, itok_B_0_7, L0_cond_W, L0_cond_Wr, L0_cond_A, L0_cond_B), L0_ffn_route_w, L0_ffn_A, L0_ffn_Bw)
    x = x + _L1_ffn_ref(_L1_cond_ref(x, itok_B_0_23, L1_cond_W, L1_cond_b, L1_cond_lora_As, L1_cond_lora_Bs), L1_ffn_W_base, L1_ffn_b_base, L1_ffn_W_router, L1_ffn_A, L1_ffn_B)
    return x

_drawn_inputs = setup_inputs


def setup_inputs(seed=0):
    import zlib

    import numpy as np

    out = dict(_drawn_inputs(seed))
    spreads = {}
    factors = {'L0_cond_Wr': 8.0,
     'L0_cond_A': 3.66,
     'L0_cond_B': 3.533,
     'L1_cond_b': 3.451,
     'L1_ffn_b_base': 3.016}
    for name, (base, spread) in spreads.items():
        noise = np.random.default_rng([zlib.crc32(name.encode()), seed]).standard_normal(out[name].shape)
        drawn = base * np.exp(spread * noise) if base else spread * noise
        out[name] = jnp.asarray(drawn.astype(out[name].dtype))
    for name, factor in factors.items():
        out[name] = (out[name] * factor).astype(out[name].dtype)
    return out
```

```python
from contextlib import ExitStack

import concourse.bass as bass
from concourse import mybir

P = 128
F32 = mybir.dt.float32
F32R = mybir.dt.float32r
U32 = mybir.dt.uint32
I32 = mybir.dt.int32
ALU = mybir.AluOpType
ACT = mybir.ActivationFunctionType



def adaln_ffn(nc, x, lang_ids, slot_ids, W0, Wr0, A0c, B0, route_w, A0f, Bw, W1, b1, lora_As, lora_Bs,
              Wb, b_base, W_router, A1, B1, out):
    NB, SEQ, D = x.shape
    T = NB * SEQ
    NT = T // P
    TPB = SEQ // P
    K = D // P
    E, R, _ = A0c.shape
    ER = E * R
    RC = E + ER
    C0C = ER + E + RC
    MC = D + RC
    MW = MC + R
    ZC = R + RC
    HALF = D // 2
    LANG_BIAS = 5.0
    GROUPS = [(0, 3), (3, 3), (6, 2)]
    assert (NB, K, E, R, TPB, ER) == (8, 8, 8, 16, 2, 128)

    xf = x.rearrange("b s d -> (b s) d")
    outf = out.rearrange("b s d -> (b s) d")
    fe_hi_dram = nc.dram_tensor("fe_hi_dram", (P + 1, MC), F32, kind="Internal").ap()
    fe_lo_dram = nc.dram_tensor("fe_lo_dram", (P + 1, MC), F32, kind="Internal").ap()

    b1_dram = nc.dram_tensor("b1_dram", (P, D), F32, kind="Internal").ap()
    x1_dram = nc.dram_tensor("x1_dram", (P, D), F32, kind="Internal").ap()

    ctx = ExitStack()
    with ctx:
        def sb(name, shape, dt=F32, where=None):
            return (where or ctx).enter_context(nc.sbuf_tensor(name, shape, dt))

        def sem(name):
            return ctx.enter_context(nc.semaphore(name))

        C0hi = sb("C0hi", [P, K, C0C], F32R)
        C0lo = sb("C0lo", [P, K, C0C], F32R)
        BwThi = sb("BwThi", [P, D], F32R)
        BwTlo = sb("BwTlo", [P, D], F32R)
        D0hi = sb("D0hi", [P, RC], F32R)
        D0lo = sb("D0lo", [P, RC], F32R)
        Ebuf = sb("Ebuf", [96, RC], F32R)
        asraw = sb("asraw", [P, K, R])
        ws_hi = [sb(f"ws_hi{i}", [P, D], F32R) for i in range(2)]
        ws_lo = [sb(f"ws_lo{i}", [P, D], F32R) for i in range(2)]
        wraw_late = [sb(f"wraw{i}", [P, D]) for i in (2, 3)]
        ident = sb("ident", [P, P])
        iota = sb("iota", [P, E])
        ids = sb("ids", [1, 2 * NB], I32)
        lang = sb("lang", [P, NB], I32)
        langf = sb("langf", [P, NB])
        bias = sb("bias", [P, NB * E])
        brow = sb("brow", [K, P])
        bcol = sb("bcol", [P, 2, K])
        hs = sb("hs", [P, 96], F32R)
        hsT = sb("hsT", [96, P], F32R)
        hg, wh, wz = sb("hg", [P, ER]), sb("wh", [P, ER]), sb("wz", [P, ER])
        hgThi, hgTlo = sb("hgThi", [P, P], F32R), sb("hgTlo", [P, P], F32R)
        whThi, whTlo = sb("whThi", [P, P], F32R), sb("whTlo", [P, P], F32R)
        wzThi, wzTlo = sb("wzThi", [P, P], F32R), sb("wzTlo", [P, P], F32R)

        def gate_tiles(n):
            return dict(lg=sb(f"lg{n}", [P, E]), mx=sb(f"mx{n}", [P, 8]), ix=sb(f"ix{n}", [P, 8], U32),
                        ixf=sb(f"ixf{n}", [P, 2]), ex=sb(f"ex{n}", [P, 1]), den=sb(f"den{n}", [P, 1]),
                        w=sb(f"w{n}", [P, 2]), ga=sb(f"ga{n}", [P, E]), gb=sb(f"gb{n}", [P, E]),
                        g=sb(f"g{n}", [P, E]))
        G0, G1, GT = gate_tiles("c"), gate_tiles("f"), gate_tiles("t")

        with ExitStack() as first:
            wraw = [sb(f"wraw{i}", [P, D], where=first) for i in (0, 1)] + wraw_late
            R0Thi, R0Tlo = sb("R0Thi", [P, K, RC], F32R, first), sb("R0Tlo", [P, K, RC], F32R, first)
            a0f, a0c = sb("a0f", [P, D], where=first), sb("a0c", [P, D], where=first)
            routers = sb("routers", [E, 2, D], where=first)
            b0raw, bwraw = sb("b0raw", [P, D], where=first), sb("bwraw", [P, D], where=first)
            bw_j, b1_j = sb("bw_j", [P, D], where=first), sb("b1_j", [P, D], where=first)
            b0hi, b0lo = sb("b0hi", [P, D], F32R, first), sb("b0lo", [P, D], F32R, first)
            xin_first, x1_first = sb("xin_first", [P, D], where=first), sb("x1_first", [P, D], where=first)
            xT_first = [sb("xThi_first", [P, D], F32R, first), sb("xTlo_first", [P, D], F32R, first)]
        Mhi = sb("Mhi", [P, K, MW], F32R)
        Mlo = sb("Mlo", [P, K, MW], F32R)

        with ExitStack() as second:
            WbThi, WbTlo = sb("WbThi", [P, K, MC], F32R, second), sb("WbTlo", [P, K, MC], F32R, second)
        B1Thi, B1Tlo = sb("B1Thi", [P, D], F32R), sb("B1Tlo", [P, D], F32R)
        x1 = [sb(f"x1_{i}", [P, D]) for i in range(2)]
        xin = [sb(f"xin{i}", [P, D]) for i in range(2)]
        xT_main = [sb("xThi", [P, D], F32R), sb("xTlo", [P, D], F32R)]
        x1T = [[sb(f"x1Thi{i}", [P, D], F32R), sb(f"x1Tlo{i}", [P, D], F32R)] for i in range(2)]
        ybuf = [sb(f"ybuf{i}", [P, HALF]) for i in range(2)]
        Fbuf = sb("Fbuf", [96, D], F32R)
        Mz = [t[:, :, D:MW] for t in (Mhi, Mlo)]

        def bank(name):
            return ctx.enter_context(nc.psum_tensor(name, [P, 512], F32))
        pm = [bank("pm0"), bank("pm1")]
        p0, p1, pt = bank("p0"), bank("p1"), bank("pt")
        big = [bank(f"big{i}") for i in range(3)]
        pt_h1, pt_hg, pt_wz, pt_wh = (pt[:, P * i:P * (i + 1)] for i in range(4))

        ident_ready = sem("ident_ready")
        gp_step = sem("gp_step")
        memsets_done = sem("memsets_done")
        bias_step = sem("bias_step")
        ids_in, lang_in, brow_in = sem("ids_in"), sem("lang_in"), sem("brow_in")
        a0f_in, a0c_in, routers_in = sem("a0f_in"), sem("a0c_in"), sem("routers_in")
        b0_in, bw_in, b1_in = sem("b0_in"), sem("bw_in"), sem("b1_in")
        bw_j_ready, b1_j_ready, b1_stored = sem("bw_j_ready"), sem("b1_j_ready"), sem("b1_stored")
        bcol_done, x1_stored, x1_back = sem("bcol_done"), sem("x1_stored"), sem("x1_back")
        x0_in = sem("x0_in")
        wraw_in = [sem(f"wraw_in{i}") for i in range(4)]
        unit_done, unit_hi, unit_lo = sem("unit_done"), sem("unit_hi"), sem("unit_lo")
        w0_hi, w0_lo, w0_used = sem("w0_hi"), sem("w0_lo"), sem("w0_used")
        b0_hi, b0_lo = sem("b0_hi"), sem("b0_lo")
        c0_hi, c0_lo = sem("c0_hi"), sem("c0_lo")
        d0w_done, d0w_hi, d0w_lo = sem("d0w_done"), sem("d0w_hi"), sem("d0w_lo")
        fe_done, fe_hi, fe_lo, fe_stored = sem("fe_done"), sem("fe_hi"), sem("fe_lo"), sem("fe_stored")
        bstat_step = sem("bstat_step")
        brow_sum = sem("brow_sum")
        w1_hi, w1_lo = sem("w1_hi"), sem("w1_lo")
        m_done, m_hi, m_lo = sem("m_done"), sem("m_hi"), sem("m_lo")
        x_in = [sem(f"x_in{i}") for i in range(2)]
        e_in, f_in, as_in = sem("e_in"), sem("f_in"), sem("as_in")
        as_hi, as_lo = sem("as_hi"), sem("as_lo")
        tx_done, xT_hi, xT_lo = sem("tx_done"), sem("xT_hi"), sem("xT_lo")
        p0_done, p1_done = sem("p0_done"), sem("p1_done")
        g0_step, g1_step, top_step = sem("g0_step"), sem("g1_step"), sem("top_step")
        lg0_ready, lg1_ready, lgt_ready, maxt_ready = (sem(n) for n in ("lg0_ready", "lg1_ready", "lgt_ready", "maxt_ready"))
        max0_ready, max1_ready = sem("max0_ready"), sem("max1_ready")
        exp0_ready, exp1_ready = sem("exp0_ready"), sem("exp1_ready")
        hg_ready, thg_done, hgT_hi, hgT_lo = sem("hg_ready"), sem("thg_done"), sem("hgT_hi"), sem("hgT_lo")
        z0_done, wh_ready, twh_done = sem("z0_done"), sem("wh_ready"), sem("twh_done")
        whT_hi, whT_lo = sem("whT_hi"), sem("whT_lo")
        xl_done, x1_ready, tx1_done = sem("xl_done"), sem("x1_ready"), sem("tx1_done")
        x1T_hi, x1T_lo = sem("x1T_hi"), sem("x1T_lo")
        hs_hi, hs_ready, ths_done, hsT_ready = sem("hs_hi"), sem("hs_ready"), sem("ths_done"), sem("hsT_ready")
        z1_done, wz_ready, twz_done = sem("z1_done"), sem("wz_ready"), sem("twz_done")
        wzT_hi, wzT_lo = sem("wzT_hi"), sem("wzT_lo")
        main_done, y_ready = sem("main_done"), sem("y_ready")
        y_out = [sem(f"y_out{i}") for i in range(2)]

        block = ctx.enter_context(nc.Block())

        def rows(t, k):
            return t[:, k * P:(k + 1) * P]

        def turn_rc(a, router, thi, tlo, c0, split, waits, router_first):
            units = []
            for k0, n in GROUPS:
                moves = []
                for j in range(n):
                    ao, ro = (j * RC + E, j * RC) if router_first else (j * RC, j * RC + ER)
                    moves += [(ao, ER, split(a, k0 + j)), (ro, E, split(router, k0 + j))]
                dst = [t[:, k0:k0 + n, c0:c0 + RC] for t in (thi, tlo)]
                units.append((moves, dst, (n * RC, "p (k c) -> p k c", dict(k=n)), 1.0, waits))
            return units

        def strided(t, j):
            return t[:, j::K]

        def by_j(t):
            return t[:, :].rearrange("p (e j r) -> p j e r", e=E, j=K)

        def j_first(t):
            return t[:, :].rearrange("p (j e r) -> p j e r", e=E, j=K)

        def turn_b(src, thi, tlo, scale, waits):
            return [([(i * P, P, rows(src, j0 + i)) for i in range(4)],
                     [t[:, :].rearrange("p (o j) -> p o j", j=K)[:, :, j0:j0 + 4] for t in (thi, tlo)],
                     (512, "p (j o) -> p o j", dict(j=4)), scale, waits) for j0 in (0, 4)]

        units_r0 = turn_rc(a0f, routers[:, 1, :], R0Thi, R0Tlo, 0, strided, [(a0f_in, 16), (routers_in, 32)], True)
        units_a0 = turn_rc(a0c, routers[:, 0, :], C0hi, C0lo, 0, rows, [(a0c_in, 16)], False)
        units_bw = turn_b(bw_j, BwThi, BwTlo, 1.0, [(bw_j_ready, 1)])
        units_b1 = turn_b(wraw[2], B1Thi, B1Tlo, 2.0, [(wraw_in[2], 16 * 10)])
        units_wb = []
        for o in range(K):
            for k0 in (0, 4):
                units_wb.append(([(i * P, P, rows(wraw[o % 4], k0 + i)) for i in range(4)],
                                 [t[:, k0:k0 + 4, o * P:(o + 1) * P] for t in (WbThi, WbTlo)],
                                 (512, "p (k c) -> p k c", dict(k=4)), 1.0,
                                 [(wraw_in[o % 4], 16 * (3 + o // 4))]))
        units_r1 = turn_rc(wraw[0], wraw[2][0:E, :], WbThi, WbTlo, D, rows, [(wraw_in[0], 80), (wraw_in[2], 80)], True)
        units_bs = [([(i * P, P, rows(wraw[1], k0 + i)) for i in range(4)],
                     [t[:, k0 * P:(k0 + 4) * P] for t in (ws_hi[0], ws_lo[0])],
                     (512, None, {}), 1.0, [(wraw_in[1], 16 * (4 + NB))]) for k0 in (0, 4)]
        units_first = units_r0 + units_a0 + units_bw
        units_second = units_wb + units_r1 + units_bs
        NU1 = len(units_first)
        NU2 = NU1 + len(units_second)

        def psum_of(q, unit):
            width, how, dims = unit[2]
            v = big[q % 3][:, 0:width]
            return v.rearrange(how, **dims) if how else v

        def split_of(hi, lo, k):
            return rows(hi, k), rows(lo, k)

        CHUNKS = [(0, 512), (512, 512), (1024, RC)]
        C0_BANKS = [pm[0], pm[1], p1]

        M_BANKS = [[pm[0], pm[1], p1], big]

        def wait_earlier(eng, s, n):
            if not isinstance(n, int) or n > 0:
                eng.wait_ge(s, n)

        @block.sync
        def _(sp):
            sp.dma_start(a0f[:, :], A0f.rearrange("e r d -> (e r) d")).then_inc(a0f_in, 16)
            sp.dma_start(routers[:, 1, :], route_w).then_inc(routers_in, 16)
            sp.dma_start(routers[:, 0, :], Wr0).then_inc(routers_in, 16)
            w0v = W0.rearrange("(p j) i -> p j i", j=K)

            def load_b(raw, src, s):
                sp.dma_start(raw[:, :].rearrange("p (e c) -> p e c", e=E),
                             src.rearrange("e (p j) r -> p e (j r)", j=K)).then_inc(s, 16)

            for j in range(K):
                if j >= 4:
                    sp.wait_ge(w0_hi, j - 3)
                    sp.wait_ge(w0_lo, j - 3)
                sp.dma_start(wraw[j % 4][:, :], w0v[:, j, :]).then_inc(wraw_in[j % 4], 16)
                if j == 1:
                    sp.dma_start(a0c[:, :], A0c.rearrange("e r d -> (e r) d")).then_inc(a0c_in, 16)
                if j == 3:
                    load_b(b0raw, B0, b0_in)
                    load_b(bwraw, Bw, bw_in)
                    sp.dma_start(xin_first[:, :], xf[0:P, :]).then_inc(x0_in, 16)
                    sp.dma_start(brow[:, :], b1.rearrange("(k p) -> k p", k=K)).then_inc(brow_in, 16)
            sp.wait_ge(b0_lo, 1)
            load_b(b0raw, B1, b1_in)
            for o in range(K):
                if o == 4:
                    sp.wait_ge(b1_j_ready, 1)
                    sp.dma_start(b1_dram, b1_j[:, :]).then_inc(b1_stored, 16)
                    sp.wait_ge(x1_ready, 2)
                    sp.dma_start(x1_dram, x1_first[:, :]).then_inc(x1_stored, 16)
                if o < 4:
                    sp.wait_ge(w0_hi, o + 5)
                    sp.wait_ge(w0_lo, o + 5)
                else:
                    sp.wait_ge(unit_done, NU1 + 2 * (o - 4) + 2)
                sp.dma_start(wraw[o % 4][:, :], Wb[o * P:(o + 1) * P, :]).then_inc(wraw_in[o % 4], 16)
            sp.wait_ge(unit_done, NU1 + 2 * 4 + 2)
            sp.dma_start(wraw[0][:, :], A1.rearrange("e r d -> (e r) d")).then_inc(wraw_in[0], 16)
            sp.wait_ge(unit_done, NU1 + 2 * 5 + 2)
            sp.wait_ge(ids_in, 32)
            for b in range(NB):
                slot = sp.value_load(ids[0:1, NB + b:NB + b + 1], min_val=0, max_val=lora_Bs.shape[0] - 1)
                sp.dma_start(wraw[1][b * R:(b + 1) * R, :],
                             lora_Bs[bass.ds(slot, 1), :, :].rearrange("s r d -> (s r) d")).then_inc(wraw_in[1], 16)
            sp.wait_ge(unit_done, NU1 + 2 * 6 + 2)
            sp.dma_start(wraw[2][0:E, :], W_router).then_inc(wraw_in[2], 16)
            w1v = W1.rearrange("(m p) i -> p m i", p=P)
            sp.wait_ge(unit_done, NU1 + 2 * K + 3)
            sp.dma_start(wraw[0][0:1, :], b_base.rearrange("(a o) -> a o", a=1)).then_inc(wraw_in[0], 16)
            for par in range(2):
                sp.dma_start(wraw[2 + par][:, :].rearrange("p (m c) -> p m c", m=K),
                             w1v[:, :, par * P:(par + 1) * P]).then_inc(wraw_in[2 + par], 16)
            sp.wait_ge(fe_hi, 3)
            sp.wait_ge(fe_lo, 3)
            sp.dma_start(fe_hi_dram[0:P, :], Mhi[:, K - 1, 0:MC].bitcast(F32)).then_inc(fe_stored, 16)
            sp.dma_start(fe_lo_dram[0:P, :], Mlo[:, K - 1, 0:MC].bitcast(F32)).then_inc(fe_stored, 16)
            sp.wait_ge(fe_hi, 6)
            sp.wait_ge(fe_lo, 6)
            sp.dma_start(fe_hi_dram[P:P + 1, :], Mhi[0:1, K - 2, 0:MC].bitcast(F32)).then_inc(fe_stored, 16)
            sp.dma_start(fe_lo_dram[P:P + 1, :], Mlo[0:1, K - 2, 0:MC].bitcast(F32)).then_inc(fe_stored, 16)
            with sp.Fori(0, K // 2 - 1) as i:
                for par in range(2):
                    sp.wait_ge(w1_hi, i * 2 + par + 1)
                    sp.wait_ge(w1_lo, i * 2 + par + 1)
                    sp.dma_start(wraw[2 + par][:, :].rearrange("p (m c) -> p m c", m=K),
                                 w1v[:, :, bass.ds((i * 2 + 2 + par) * P, P)]).then_inc(wraw_in[2 + par], 16)

            blocks = [(0, fe_hi_dram), (32, fe_lo_dram), (64, fe_hi_dram)]

            def load_e(b):
                for p, src in blocks:
                    sp.dma_start(Ebuf[p:p + R, :].bitcast(F32), src[bass.ds(b * R, R), D:MC]).then_inc(e_in, 16)

            def load_f(b):
                for p, src in blocks:
                    sp.dma_start(Fbuf[p:p + R, :].bitcast(F32), src[bass.ds(b * R, R), 0:D]).then_inc(f_in, 16)

            def load_as(b, guard):
                slot = sp.value_load(ids[0:1, bass.ds(NB + b, 1)], min_val=0, max_val=lora_As.shape[0] - 1)
                src = lora_As[bass.ds(slot, 1), :, :].rearrange("s (k p) r -> p (s k) r", p=P)
                if guard:
                    sp.wait_ge(as_hi, b)
                    sp.wait_ge(as_lo, b)
                sp.dma_start(asraw[:, :, :], src).then_inc(as_in, 16)

            def load_x(t, turn):
                sp.dma_start(xin[turn][:, :], xf[bass.ds(t * P, P), :]).then_inc(x_in[turn], 16)

            sp.wait_ge(w1_hi, K - 1)
            sp.wait_ge(w1_lo, K - 1)
            sp.wait_ge(b1_stored, 16)
            sp.dma_start(wraw[2][:, :], b1_dram).then_inc(wraw_in[2], 16)
            sp.wait_ge(w1_hi, K)
            sp.wait_ge(w1_lo, K)
            sp.wait_ge(x1_stored, 16)
            sp.dma_start(wraw[3][:, :], x1_dram).then_inc(wraw_in[3], 16)
            load_as(0, False)
            sp.wait_ge(m_done, 3 * K)
            load_x(1, 1)
            sp.dma_start(x1[0][:, :], x1_dram).then_inc(x1_back, 16)
            sp.wait_ge(fe_stored, 64)
            sp.wait_ge(memsets_done, 3)
            load_e(0)
            load_f(0)
            for p, src in blocks[0:2]:
                sp.dma_start(Ebuf[p + R:p + R + 1, :].bitcast(F32), src[P:P + 1, D:MC]).then_inc(e_in, 16)
                sp.dma_start(Fbuf[p + R:p + R + 1, :].bitcast(F32), src[P:P + 1, 0:D]).then_inc(f_in, 16)

            def slot_dmas(m, par, b, last, more_x):
                if more_x:
                    sp.wait_ge(x1_ready, m * 2 + 2)
                    load_x(m + 2, par)
                if par == 0 and not last:
                    load_as(b + 1, True)
                if par == 1 and not last:
                    sp.wait_ge(z1_done, m + 1)
                    load_e(b + 1)
                for h in range(2):
                    sp.wait_ge(y_ready, m * 2 + h + 1)
                    sp.dma_start(outf[bass.ds(m * P, P), h * HALF:(h + 1) * HALF], ybuf[h][:, :]).then_inc(y_out[h], 16)
                if par == 1 and not last:
                    sp.wait_ge(fe_stored, 64)
                    sp.wait_ge(main_done, m * 2 + 2)
                    load_f(b + 1)

            for par in range(2):
                slot_dmas(par, par, 0, False, True)
            with sp.Fori(1, NB - 1) as i:
                for par in range(2):
                    slot_dmas(i * 2 + par, par, i, False, True)
            for par in range(2):
                slot_dmas(NT - 2 + par, par, NB - 1, True, False)
            for h in range(2):
                sp.wait_ge(y_out[h], 16 * NT)

        @block.gpsimd
        def _(gp):
            gp.memset(ident[:, :], 0.0).then_inc(gp_step, 1)
            gp.wait_ge(gp_step, 1)
            gp.affine_select(out=ident[:, :], in_=ident[:, :], compare_op=ALU.not_equal, fill=1.0,
                             base=0, pattern=[[-1, P]], channel_multiplier=1).then_inc(ident_ready, 1)
            gp.dma_start(ids[0:1, 0:NB], lang_ids.rearrange("(a b) -> a b", a=1)).then_inc(ids_in, 16)
            gp.dma_start(ids[0:1, NB:2 * NB], slot_ids.rearrange("(a b) -> a b", a=1)).then_inc(ids_in, 16)
            gp.dma_start(lang[:, :], lang_ids.rearrange("(a b) -> a b", a=1).broadcast_to([P, NB])).then_inc(lang_in, 16)
            gp.iota(iota[:, :], pattern=[[1, E]], base=0, channel_multiplier=0,
                    allow_small_or_imprecise_dtypes=True).then_inc(gp_step, 1)
            gp.wait_ge(bw_in, 16)
            gp.tensor_copy(j_first(bw_j), by_j(bwraw)).then_inc(bw_j_ready, 1)
            gp.wait_ge(b1_in, 16)
            gp.tensor_copy(j_first(b1_j), by_j(b0raw)).then_inc(b1_j_ready, 1)

        @block.scalar
        def _(act):
            def copy_units(q0, units):
                for q, unit in enumerate(units, q0):
                    act.wait_ge(unit_done, q + 1)
                    act.activation(unit[1][0], psum_of(q, unit), ACT.Copy, scale=unit[3]).then_inc(unit_hi, 1)

            def hi_half(done, nth, dst, src, ready):
                act.wait_ge(done, nth)
                act.activation(dst, src, ACT.Copy).then_inc(ready, 1)

            copy_units(0, units_r0)
            for j in range(K):
                act.wait_ge(wraw_in[j % 4], 16 * (j // 4 + 1))
                if j >= 2:
                    act.wait_ge(w0_used, j - 1)
                act.activation(ws_hi[j % 2][:, :], wraw[j % 4][:, :], ACT.Copy).then_inc(w0_hi, 1)
                if j == 1:
                    copy_units(3, units_a0)
                if j == 5:
                    act.wait_ge(b0_in, 16)
                    act.activation(j_first(b0hi), by_j(b0raw), ACT.Copy).then_inc(b0_hi, 1)
            copy_units(6, units_bw)
            act.wait_ge(w0_used, K)
            for g, (k0, n) in enumerate(GROUPS):
                act.activation(C0hi[:, k0:k0 + n, ER + E:C0C],
                               C0_BANKS[g][:, 0:n * RC].rearrange("p (k c) -> p k c", k=n), ACT.Copy).then_inc(c0_hi, 1)
            act.wait_ge(d0w_done, 1)
            act.activation(D0hi[:, :], p0[:, 0:RC], ACT.Copy, scale=2.0).then_inc(d0w_hi, 1)

            def xT_part(t, xT):
                wait_earlier(act, p0_done, t)
                for h in range(2):
                    hi_half(tx_done, t * 2 + h + 1, xT[0][:, h * HALF:(h + 1) * HALF], big[1 + h][:, :], xT_hi)

            def exp0(t):
                act.wait_ge(max0_ready, t + 1)
                act.activation(G0["ex"][:, :], G0["mx"][:, 0:1], ACT.Exp, bias=G0["mx"][:, 1:2], scale=-1.0)\
                   .then_inc(exp0_ready, 1)

            def exp1(t):
                act.wait_ge(max1_ready, t + 1)
                act.activation(G1["ex"][:, :], G1["mx"][:, 0:1], ACT.Exp, bias=G1["mx"][:, 1:2], scale=-1.0)\
                   .then_inc(exp1_ready, 1)

            def hgT_part(t):
                wait_earlier(act, z0_done, t)
                hi_half(thg_done, t + 1, hgThi[:, :], pt_hg, hgT_hi)

            def whT_part(t):
                wait_earlier(act, xl_done, t * 2)
                hi_half(twh_done, t + 1, whThi[:, :], pt_wh, whT_hi)

            def x1T_part(t, turn):
                wait_earlier(act, main_done, t * 2 - 2)
                for h in range(2):
                    hi_half(tx1_done, t * 2 + h + 1, x1T[turn][0][:, h * HALF:(h + 1) * HALF],
                            big[2 - 2 * h][:, :], x1T_hi)

            def hsT_part(t):
                wait_earlier(act, main_done, t * 2)
                hi_half(ths_done, t + 1, hsT[:, :], pt_h1[0:96, :], hsT_ready)

            def wzT_part(t):
                wait_earlier(act, main_done, t * 2)
                hi_half(twz_done, t + 1, wzThi[:, :], pt_wz, wzT_hi)

            def as_part(b):
                act.wait_ge(as_in, b * 16 + 16)
                wait_earlier(act, p1_done, b * 2)
                act.activation(Mhi[:, :, MC:MW], asraw[:, :, :], ACT.Copy).then_inc(as_hi, 1)

            xT_part(0, xT_first)
            exp0(0)
            hgT_part(0)
            whT_part(0)

            copy_units(NU1, units_second)
            act.wait_ge(x1_stored, 16)
            for c, (c0, n) in enumerate(CHUNKS):
                act.wait_ge(fe_done, c + 1)
                act.activation(Mhi[:, K - 1, c0:c0 + n], [pm[0], pm[1], p1][c][:, 0:n], ACT.Copy, scale=2.0)\
                   .then_inc(fe_hi, 1)
            for c, (c0, n) in enumerate(CHUNKS):
                act.wait_ge(brow_sum, c + 1)
                act.activation(Mhi[0:1, K - 2, c0:c0 + n], wraw[1][0:1, 0:n] if c == 2 else wraw[0][0:1, c0:c0 + n],
                               ACT.Copy).then_inc(fe_hi, 1)
            act.wait_ge(fe_stored, 64)

            def keep_m(i, par):
                for c, (c0, n) in enumerate(CHUNKS):
                    act.wait_ge(m_done, i * 6 + par * 3 + c + 1)
                    act.activation(Mhi[:, bass.ds(i * 2 + par, 1), c0:c0 + n],
                                   M_BANKS[par][c][:, 0:n].unsqueeze(1), ACT.Copy).then_inc(m_hi, 1)

            act.wait_ge(wraw_in[2], 96)
            act.wait_ge(fe_done, 6)
            act.activation(ws_hi[0][:, :], wraw[2][:, :], ACT.Copy).then_inc(w1_hi, 1)
            act.wait_ge(wraw_in[3], 80)
            act.activation(ws_hi[1][:, :], wraw[3][:, :], ACT.Copy).then_inc(w1_hi, 1)
            with act.Fori(0, K // 2 - 1) as i:
                for par in range(2):
                    keep_m(i, par)
                    act.wait_ge(wraw_in[2 + par], i * 16 + 16 * (7 - par))
                    act.activation(ws_hi[par][:, :], wraw[2 + par][:, :], ACT.Copy).then_inc(w1_hi, 1)
            for par in range(2):
                keep_m(K // 2 - 1, par)

            copy_units(NU2, units_b1)
            as_part(0)
            x1T_part(0, 0)
            xT_part(1, xT_main)

            def slot(m, par, b, has_a, has_n):
                if has_a:
                    exp0(m + 1)
                hsT_part(m)
                if has_a:
                    hgT_part(m + 1)
                exp1(m)
                wzT_part(m)
                if has_a:
                    whT_part(m + 1)
                    x1T_part(m + 1, 1 - par)
                if has_n:
                    xT_part(m + 2, xT_main)
                if par == 1 and has_n:
                    as_part(b + 1)
            for par in range(2):
                slot(par, par, 0, True, True)
            with act.Fori(1, NB - 1) as i:
                for par in range(2):
                    slot(i * 2 + par, par, i, True, True)
            slot(NT - 2, 0, NB - 1, True, False)
            slot(NT - 1, 1, NB - 1, False, False)

        @block.vector
        def _(dve):
            def lo(out_, src, hi, scale=1.0):
                return dve.scalar_tensor_tensor(out=out_, in0=src, scalar=scale, in1=hi.bitcast(F32),
                                                op0=ALU.mult, op1=ALU.subtract)

            def lo_units(q0, units):
                for q, unit in enumerate(units, q0):
                    dve.wait_ge(unit_hi, q + 1)
                    lo(unit[1][1], psum_of(q, unit), unit[1][0], unit[3]).then_inc(unit_lo, 1)

            dve.memset(hs[:, :].bitcast(F32), 0.0).then_inc(bias_step, 1)
            dve.memset(Ebuf[:, :].bitcast(F32), 0.0).then_inc(memsets_done, 1)
            dve.wait_ge(bias_step, 1)
            dve.memset(hs[:, R:R + 1].bitcast(F32), 1.0).then_inc(memsets_done, 1)
            dve.memset(hs[:, 32 + R:32 + R + 1].bitcast(F32), 1.0).then_inc(bias_step, 1)
            lo_units(0, units_r0)
            for j in range(K):
                dve.wait_ge(w0_hi, j + 1)
                if j >= 2:
                    dve.wait_ge(w0_used, j - 1)
                lo(ws_lo[j % 2][:, :], wraw[j % 4][:, :], ws_hi[j % 2][:, :]).then_inc(w0_lo, 1)
                if j == 1:
                    lo_units(3, units_a0)
                if j == 5:
                    dve.wait_ge(b0_hi, 1)
                    for j in range(K):
                        ins = lo(j_first(b0lo)[:, j], by_j(b0raw)[:, j], j_first(b0hi)[:, j])
                    ins.then_inc(b0_lo, 1)
            lo_units(6, units_bw)
            dve.wait_ge(lang_in, 16)
            dve.tensor_copy(langf[:, :], lang[:, :]).then_inc(bias_step, 1)
            dve.wait_ge(bias_step, 3)
            dve.wait_ge(gp_step, 2)
            for b in range(NB):
                dve.tensor_scalar(bias[:, b * E:(b + 1) * E], iota[:, :], langf[:, b:b + 1], LANG_BIAS,
                                  ALU.is_equal, ALU.mult).then_inc(bias_step, 1)
            for g, (k0, n) in enumerate(GROUPS):
                dve.wait_ge(c0_hi, g + 1)
                lo(C0lo[:, k0:k0 + n, ER + E:C0C], C0_BANKS[g][:, 0:n * RC].rearrange("p (k c) -> p k c", k=n),
                   C0hi[:, k0:k0 + n, ER + E:C0C]).then_inc(c0_lo, 1)
            dve.wait_ge(d0w_hi, 1)
            lo(D0lo[:, :], p0[:, 0:RC], D0hi[:, :], 2.0).then_inc(d0w_lo, 1)

            def xT_part(t, xT):
                for h in range(2):
                    dve.wait_ge(xT_hi, t * 2 + h + 1)
                    s = slice(h * HALF, (h + 1) * HALF)
                    lo(xT[1][:, s], big[1 + h][:, :], xT[0][:, s]).then_inc(xT_lo, 1)

            G_STEPS = 8

            def iota_there():
                dve.wait_ge(gp_step, 2)

            def spread(out_, h, g):
                return dve.tensor_tensor(out_.rearrange("p (e r) -> p e r", e=E), h.rearrange("p (e r) -> p e r", e=E),
                                         g[:, :].unsqueeze(2).broadcast_to([P, E, R]), ALU.mult)

            def gates0(t, b):
                dve.wait_ge(p0_done, t + 1)
                dve.tensor_tensor(G0["lg"][:, :], p0[:, ER:ER + E], bias[:, bass.ds(b * E, E)], ALU.add).then_inc(lg0_ready, 1)
                iota_there()
                dve.wait_ge(lg0_ready, t + 1)
                gates_from(G0, G0["lg"][:, :], t, g0_step, max0_ready, exp0_ready)
                wait_earlier(dve, thg_done, t)
                spread(hg[:, :], p0[:, 0:ER], G0["g"]).then_inc(hg_ready, 1)

            def gates_from(G, logits, t, step, max_ready, exp_ready):
                def at(n):
                    dve.wait_ge(step, t * G_STEPS + n)
                dve.max(G["mx"][:, :], logits).then_inc(max_ready, 1)
                iota_there()
                dve.wait_ge(max_ready, t + 1)
                dve.max_index(G["ix"][:, :], G["mx"][:, :], logits).then_inc(step, 1)
                at(1)
                dve.tensor_copy(G["ixf"][:, :], G["ix"][:, 0:2]).then_inc(step, 1)
                dve.wait_ge(exp_ready, t + 1)
                dve.tensor_scalar(G["den"][:, :], G["ex"][:, :], 1.0, None, ALU.add).then_inc(step, 1)
                at(3)
                dve.reciprocal(G["w"][:, 0:1], G["den"][:, :]).then_inc(step, 1)
                at(4)
                dve.tensor_tensor(G["w"][:, 1:2], G["ex"][:, :], G["w"][:, 0:1], ALU.mult).then_inc(step, 1)
                dve.tensor_scalar(G["ga"][:, :], iota[:, :], G["ixf"][:, 0:1], G["w"][:, 0:1],
                                  ALU.is_equal, ALU.mult).then_inc(step, 1)
                at(5)
                dve.tensor_scalar(G["gb"][:, :], iota[:, :], G["ixf"][:, 1:2], G["w"][:, 1:2],
                                  ALU.is_equal, ALU.mult).then_inc(step, 1)
                at(7)
                dve.tensor_tensor(G["g"][:, :], G["ga"][:, :], G["gb"][:, :], ALU.add).then_inc(step, 1)
                at(8)

            def gates1(t):
                dve.wait_ge(z1_done, t + 1)
                dve.tensor_copy(G1["lg"][:, :], p1[:, 0:E]).then_inc(lg1_ready, 1)
                iota_there()
                dve.wait_ge(lg1_ready, t + 1)
                gates_from(G1, G1["lg"][:, :], t, g1_step, max1_ready, exp1_ready)
                wait_earlier(dve, twz_done, t)
                spread(wz[:, :], p1[:, E:RC], G1["g"]).then_inc(wz_ready, 1)

            def top1(t):
                TOP = 3

                def at(n):
                    dve.wait_ge(top_step, t * TOP + n)
                z = ER + E
                dve.wait_ge(z0_done, t + 1)
                dve.tensor_copy(GT["lg"][:, :], p0[:, z:z + E]).then_inc(lgt_ready, 1)
                iota_there()
                dve.wait_ge(lgt_ready, t + 1)
                dve.max(GT["mx"][:, :], GT["lg"][:, :]).then_inc(maxt_ready, 1)
                iota_there()
                dve.wait_ge(maxt_ready, t + 1)
                dve.max_index(GT["ix"][:, :], GT["mx"][:, :], GT["lg"][:, :]).then_inc(top_step, 1)
                at(1)
                dve.tensor_copy(GT["ixf"][:, :], GT["ix"][:, 0:2]).then_inc(top_step, 1)
                at(2)
                dve.tensor_scalar(GT["g"][:, :], iota[:, :], GT["ixf"][:, 0:1], GT["mx"][:, 0:1],
                                  ALU.is_equal, ALU.mult).then_inc(top_step, 1)
                at(3)
                wait_earlier(dve, twh_done, t)
                spread(wh[:, :], p0[:, z + E:C0C], GT["g"]).then_inc(wh_ready, 1)

            def hgT_part(t):
                dve.wait_ge(hgT_hi, t + 1)
                lo(hgTlo[:, :], pt_hg, hgThi[:, :]).then_inc(hgT_lo, 1)

            def whT_part(t):
                dve.wait_ge(whT_hi, t + 1)
                lo(whTlo[:, :], pt_wh, whThi[:, :]).then_inc(whT_lo, 1)

            def wzT_part(t):
                dve.wait_ge(wzT_hi, t + 1)
                lo(wzTlo[:, :], pt_wz, wzThi[:, :]).then_inc(wzT_lo, 1)

            def x1_part(t, dst, src):
                wait_earlier(dve, tx1_done, t * 2 - 2)
                for h in range(2):
                    dve.wait_ge(xl_done, t * 2 + h + 1)
                    s = slice(h * HALF, (h + 1) * HALF)
                    dve.tensor_tensor(dst[:, s], big[h][:, :], src[:, s], ALU.add).then_inc(x1_ready, 1)

            def x1T_part(t, turn):
                for h in range(2):
                    dve.wait_ge(x1T_hi, t * 2 + h + 1)
                    s = slice(h * HALF, (h + 1) * HALF)
                    lo(x1T[turn][1][:, s], big[2 - 2 * h][:, :], x1T[turn][0][:, s]).then_inc(x1T_lo, 1)

            def hs_part(t):
                dve.wait_ge(p1_done, t + 1)
                wait_earlier(dve, ths_done, t)
                dve.tensor_copy(hs[:, 0:64].rearrange("p (b c) -> p b c", b=2)[:, :, 0:R],
                                p1[:, RC:ZC].unsqueeze(1).broadcast_to([P, 2, R])).then_inc(hs_hi, 1)
                dve.wait_ge(hs_hi, t + 1)
                lo(hs[:, 64:64 + R], p1[:, RC:ZC], hs[:, 0:R]).then_inc(hs_ready, 1)

            def y_part(t, turn, h):
                dve.wait_ge(main_done, t * 2 + h + 1)
                wait_earlier(dve, y_out[h], t * 16)
                s = slice(h * HALF, (h + 1) * HALF)
                dve.tensor_tensor(ybuf[h][:, :], pm[h][:, :], x1[turn][:, s], ALU.add).then_inc(y_ready, 1)

            def as_part(b):
                dve.wait_ge(as_hi, b + 1)
                lo(Mlo[:, :, MC:MW], asraw[:, :, :], Mhi[:, :, MC:MW]).then_inc(as_lo, 1)

            dve.wait_ge(bias_step, 3 + NB)
            xT_part(0, xT_first)
            gates0(0, 0)
            hgT_part(0)
            top1(0)
            whT_part(0)
            x1_part(0, x1_first, xin_first)

            lo_units(NU1, units_second)
            dve.wait_ge(w0_used, K)
            dve.memset(ws_hi[1][:, :].bitcast(F32), 0.0).then_inc(bstat_step, 1)
            dve.memset(ws_lo[1][:, :].bitcast(F32), 0.0).then_inc(bstat_step, 1)
            dve.wait_ge(bcol_done, 1)
            dve.wait_ge(bstat_step, 2)
            bh = ws_hi[1][:, :].rearrange("p (k c) -> p k c", k=K)[:, :, 0:1]
            bl = ws_lo[1][:, :].rearrange("p (k c) -> p k c", k=K)[:, :, 0:1]
            bp = pt[:, 0:K].unsqueeze(2)
            dve.tensor_copy(bh, bp).then_inc(bstat_step, 1)
            dve.wait_ge(bstat_step, 3)
            lo(bl, bp, bh).then_inc(bstat_step, 1)
            for c, (c0, n) in enumerate(CHUNKS):
                dve.wait_ge(fe_hi, c + 1)
                lo(Mlo[:, K - 1, c0:c0 + n], [pm[0], pm[1], p1][c][:, 0:n], Mhi[:, K - 1, c0:c0 + n], 2.0)\
                    .then_inc(fe_lo, 1)
            dve.wait_ge(wraw_in[0], 96)
            for c, (c0, n) in enumerate(CHUNKS):
                dve.wait_ge(fe_done, 4 + c)
                if c < 2:
                    row = wraw[0][0:1, c0:c0 + n]
                    dve.tensor_tensor(row, big[c][0:1, 0:n], row, ALU.add).then_inc(brow_sum, 1)
                else:
                    dve.tensor_copy(wraw[1][0:1, 0:n], big[c][0:1, 0:n]).then_inc(brow_sum, 1)
            for c, (c0, n) in enumerate(CHUNKS):
                dve.wait_ge(fe_hi, 4 + c)
                lo(Mlo[0:1, K - 2, c0:c0 + n], wraw[1][0:1, 0:n] if c == 2 else wraw[0][0:1, c0:c0 + n],
                   Mhi[0:1, K - 2, c0:c0 + n]).then_inc(fe_lo, 1)
            dve.wait_ge(fe_stored, 64)

            def keep_m(i, par):
                for c, (c0, n) in enumerate(CHUNKS):
                    dve.wait_ge(m_hi, i * 6 + par * 3 + c + 1)
                    lo(Mlo[:, bass.ds(i * 2 + par, 1), c0:c0 + n], M_BANKS[par][c][:, 0:n].unsqueeze(1),
                       Mhi[:, bass.ds(i * 2 + par, 1), c0:c0 + n]).then_inc(m_lo, 1)

            for par in range(2):
                dve.wait_ge(w1_hi, par + 1)
                lo(ws_lo[par][:, :], wraw[2 + par][:, :], ws_hi[par][:, :]).then_inc(w1_lo, 1)
            with dve.Fori(0, K // 2 - 1) as i:
                for par in range(2):
                    keep_m(i, par)
                    dve.wait_ge(w1_hi, i * 2 + 3 + par)
                    lo(ws_lo[par][:, :], wraw[2 + par][:, :], ws_hi[par][:, :]).then_inc(w1_lo, 1)
            for par in range(2):
                keep_m(K // 2 - 1, par)

            dve.wait_ge(m_done, 3 * K)
            dve.memset(Fbuf[:, :].bitcast(F32), 0.0).then_inc(memsets_done, 1)
            lo_units(NU2, units_b1)
            as_part(0)
            x1T_part(0, 0)
            xT_part(1, xT_main)
            dve.wait_ge(x1_back, 16)

            def slot(m, par, b, has_a, has_n):
                hs_part(m)
                if has_a:
                    gates0(m + 1, b + par)
                    hgT_part(m + 1)
                gates1(m)
                if has_a:
                    top1(m + 1)
                wzT_part(m)
                if has_a:
                    whT_part(m + 1)
                y_part(m, par, 0)
                if has_a:
                    x1_part(m + 1, x1[1 - par], xin[1 - par])
                    x1T_part(m + 1, 1 - par)
                if has_n:
                    xT_part(m + 2, xT_main)
                if par == 1 and has_n:
                    as_part(b + 1)
                y_part(m, par, 1)
            for par in range(2):
                slot(par, par, 0, True, True)
            with dve.Fori(1, NB - 1) as i:
                for par in range(2):
                    slot(i * 2 + par, par, i, True, True)
            slot(NT - 2, 0, NB - 1, True, False)
            slot(NT - 1, 1, NB - 1, False, False)

        @block.tensor
        def _(pe):
            def turn_units(q0, units):
                for q, unit in enumerate(units, q0):
                    for s, v in unit[4]:
                        pe.wait_ge(s, v)
                    if q >= 3:
                        pe.wait_ge(unit_lo, q - 2)
                    moves = unit[0]
                    for n, (col, width, src) in enumerate(moves):
                        kp = src.shape[0]
                        ins = pe.transpose(big[q % 3][:, col:col + width], src, ident[0:kp, 0:kp])
                    ins.then_inc(unit_done, 1)

            def three(out_, l, r, start, stop, **kw):
                pe.matmul(out_, l[0], r[0], start=start, stop=False, **kw)
                pe.matmul(out_, l[0], r[1], start=False, stop=False, **kw)
                return pe.matmul(out_, l[1], r[0], start=False, stop=stop, **kw)

            pe.wait_ge(ident_ready, 1)
            turn_units(0, units_r0)
            pe.wait_ge(unit_lo, 3)
            for j in range(K):
                if j == 1:
                    turn_units(3, units_a0)
                pe.wait_ge(w0_lo, j + 1)
                for k in range(K):
                    g = min(k // 3, 2)
                    c = (k - GROUPS[g][0]) * RC
                    ins = three(C0_BANKS[g][:, c:c + RC], split_of(ws_hi[j % 2], ws_lo[j % 2], k),
                                (R0Thi[:, j, :], R0Tlo[:, j, :]), j == 0 and c == 0, j == K - 1,
                                skip_group_check=True)
                ins.then_inc(w0_used, 1)
            turn_units(6, units_bw)
            pe.wait_ge(b0_lo, 1)
            for j in range(K):
                ins = three(p0[:, 0:RC], split_of(b0hi, b0lo, j), (R0Thi[:, j, :], R0Tlo[:, j, :]),
                            j == 0, j == K - 1)
            ins.then_inc(d0w_done, 1)

            def turn_x(t, src):
                for h in range(2):
                    for k in range(4):
                        ins = pe.transpose(rows(big[1 + h], k), rows(src, 4 * h + k), ident[:, :])
                    ins.then_inc(tx_done, 1)

            def small0(t, xT):
                pe.wait_ge(xT_lo, t * 2 + 2)
                for k in range(K):
                    ins = three(p0[:, 0:C0C], split_of(xT[0], xT[1], k), (C0hi[:, k, :], C0lo[:, k, :]),
                                k == 0, k == K - 1, skip_group_check=True)
                ins.then_inc(p0_done, 1)

            def turn_small(s, nth, dst, src, done):
                pe.wait_ge(s, nth)
                pe.transpose(dst, src, ident[:, :]).then_inc(done, 1)

            def add_lora0(t):
                pe.wait_ge(hgT_lo, t + 1)
                three(p0[:, ER + E:C0C], (hgThi[:, :], hgTlo[:, :]), (D0hi[:, :], D0lo[:, :]), False, True,
                      skip_group_check=True).then_inc(z0_done, 1)

            def ffn0(t, guard):
                pe.wait_ge(whT_lo, t + 1)
                for h in range(2):
                    if guard:
                        if h == 0:
                            pe.wait_ge(x1T_lo, t * 2)
                        else:
                            pe.wait_ge(xT_lo, t * 2 + 1)
                    s = slice(h * HALF, (h + 1) * HALF)
                    three(big[h][:, :], (whThi[:, :], whTlo[:, :]), (BwThi[:, s], BwTlo[:, s]), True, True)\
                        .then_inc(xl_done, 1)

            def turn_x1(t, src):
                for h in range(2):
                    if h == 0:
                        pe.wait_ge(xT_lo, t * 2 + 2)
                        pe.wait_ge(x1_ready, t * 2 + 1)
                    else:
                        pe.wait_ge(x1_ready, t * 2 + 2)
                    for k in range(4):
                        ins = pe.transpose(rows(big[2 - 2 * h], k), rows(src, 4 * h + k), ident[:, :])
                    ins.then_inc(tx1_done, 1)

            def turn_x_main(t, turn, nth):
                pe.wait_ge(x_in[turn], nth * 16)
                for h in range(2):
                    if h == 0:
                        pe.wait_ge(x1_ready, t * 2)
                    else:
                        pe.wait_ge(x1T_lo, t * 2 - 1)
                    for k in range(4):
                        ins = pe.transpose(rows(big[1 + h], k), rows(xin[turn], 4 * h + k), ident[:, :])
                    ins.then_inc(tx_done, 1)

            pe.wait_ge(x0_in, 16)
            pe.wait_ge(unit_lo, NU1)
            turn_x(0, xin_first)
            pe.wait_ge(c0_lo, 3)
            pe.wait_ge(d0w_lo, 1)
            small0(0, xT_first)
            turn_small(hg_ready, 1, pt_hg, hg[:, :], thg_done)
            add_lora0(0)
            turn_small(wh_ready, 1, pt_wh, wh[:, :], twh_done)
            ffn0(0, False)
            pe.wait_ge(x1_ready, 2)

            turn_units(NU1, units_second)
            pe.wait_ge(brow_in, 16)
            pe.transpose(pt[:, 0:K], brow[:, :], ident[0:K, 0:K]).then_inc(bcol_done, 1)
            pe.wait_ge(unit_lo, NU2)
            for c, (c0, n) in enumerate(CHUNKS):
                for k in range(K):
                    ins = three([pm[0], pm[1], p1][c][:, 0:n], split_of(ws_hi[0], ws_lo[0], k),
                                (WbThi[:, k, c0:c0 + n], WbTlo[:, k, c0:c0 + n]), k == 0, k == K - 1)
                ins.then_inc(fe_done, 1)
            pe.wait_ge(bstat_step, 4)
            for c, (c0, n) in enumerate(CHUNKS):
                for k in range(K):
                    ins = three(big[c][:, 0:n], split_of(ws_hi[1], ws_lo[1], k),
                                (WbThi[:, k, c0:c0 + n], WbTlo[:, k, c0:c0 + n]), k == 0, k == K - 1)
                ins.then_inc(fe_done, 1)

            pe.wait_ge(fe_lo, 3)
            pe.wait_ge(brow_sum, 3)

            def m_tile(i, par, guard):
                pe.wait_ge(w1_lo, i * 2 + par + 1)
                for c, (c0, n) in enumerate(CHUNKS):
                    if guard:
                        pe.wait_ge(m_lo, i * 6 + par * 3 + c - 5)
                    for k in range(K):
                        ins = three(M_BANKS[par][c][:, 0:n], split_of(ws_hi[par], ws_lo[par], k),
                                    (WbThi[:, k, c0:c0 + n], WbTlo[:, k, c0:c0 + n]), k == 0, k == K - 1)
                    ins.then_inc(m_done, 1)
            for par in range(2):
                m_tile(0, par, False)
            with pe.Fori(1, K // 2) as i:
                for par in range(2):
                    m_tile(i, par, True)

            pe.wait_ge(m_lo, 3 * K)
            pe.wait_ge(memsets_done, 3)
            pe.wait_ge(bias_step, 3)
            turn_units(NU2, units_b1)
            pe.wait_ge(wraw_in[3], 16 * 9)
            pe.wait_ge(unit_lo, NU2 + 2)
            turn_x1(0, wraw[3])
            turn_x_main(1, 1, 1)

            def slot(m, par, b, has_a, has_n):
                a, n = m + 1, m + 2
                xa = x1T[par]

                def main(c):
                    h, k0 = c // 4, c % 4 * 2
                    for k in (k0, k0 + 1):
                        s = slice(h * HALF, (h + 1) * HALF)
                        three(pm[h][:, :], split_of(xa[0], xa[1], k), (Mhi[:, k, s], Mlo[:, k, s]), k == 0, False)

                def lora(h):
                    s = slice(h * HALF, (h + 1) * HALF)
                    three(pm[h][:, :], (wzThi[:, :], wzTlo[:, :]), (B1Thi[:, s], B1Tlo[:, s]), False, False)
                    pe.matmul(pm[h][:, :], hsT[:, :], Fbuf[:, s], start=False, stop=True).then_inc(main_done, 1)

                pe.wait_ge(x1T_lo, m * 2 + 2)
                pe.wait_ge(as_lo, b + 1)
                for k in range(K):
                    ins = three(p1[:, 0:ZC], split_of(xa[0], xa[1], k), (Mz[0][:, k, :], Mz[1][:, k, :]),
                                k == 0, k == K - 1, skip_group_check=True)
                ins.then_inc(p1_done, 1)
                if has_a:
                    small0(a, xT_main)
                main(0)
                turn_small_hs(m)
                main(1)
                pe.wait_ge(hsT_ready, m + 1)
                pe.wait_ge(e_in, b * 48 + 48 + 32)
                pe.matmul(p1[:, 0:RC], hsT[:, :], Ebuf[:, :], start=False, stop=True,
                          skip_group_check=True).then_inc(z1_done, 1)
                if has_a:
                    turn_small(hg_ready, a + 1, pt_hg, hg[:, :], thg_done)
                main(2)
                if has_a:
                    add_lora0(a)
                main(3)
                turn_small(wz_ready, m + 1, pt_wz, wz[:, :], twz_done)
                main(4)
                pe.wait_ge(wzT_lo, m + 1)
                if has_a:
                    turn_small(wh_ready, a + 1, pt_wh, wh[:, :], twh_done)
                pe.wait_ge(f_in, b * 48 + 48 + 32)
                lora(0)
                main(5)
                if has_a:
                    ffn0(a, True)
                main(6)
                if has_a:
                    turn_x1(a, x1[1 - par])
                main(7)
                if has_n:
                    turn_x_main(n, par, (b + 1) + (1 if par == 1 else 0))
                lora(1)

            def turn_small_hs(m):
                pe.wait_ge(hs_ready, m + 1)
                pe.transpose(pt_h1[0:96, :], hs[:, :].bitcast(F32), ident[:, :]).then_inc(ths_done, 1)

            for par in range(2):
                slot(par, par, 0, True, True)
            with pe.Fori(1, NB - 1) as i:
                for par in range(2):
                    slot(i * 2 + par, par, i, True, True)
            slot(NT - 2, 0, NB - 1, True, False)
            slot(NT - 1, 1, NB - 1, False, False)


_INS = ['x', 'itok_B_0_7', 'itok_B_0_23', 'L0_cond_W', 'L0_cond_Wr', 'L0_cond_A', 'L0_cond_B', 'L0_ffn_route_w',
        'L0_ffn_A', 'L0_ffn_Bw', 'L1_cond_W', 'L1_cond_b', 'L1_cond_lora_As', 'L1_cond_lora_Bs', 'L1_ffn_W_base',
        'L1_ffn_b_base', 'L1_ffn_W_router', 'L1_ffn_A', 'L1_ffn_B']


def kernel(**inputs):
    import numpy as _np
    import concourse.bacc as _bacc
    from concourse import mybir as _mybir
    from concourse.bass_utils import run_bass_kernel_spmd as _run

    nc = _bacc.Bacc("TRN2", target_bir_lowering=False, num_devices=1)
    arrays, args = {}, []
    for name in _INS:
        a = _np.ascontiguousarray(inputs[name])
        arrays[f"in_{name}_dram"] = a
        args.append(nc.dram_tensor(f"in_{name}_dram", a.shape, _mybir.dt.from_np(a.dtype), kind="ExternalInput").ap())
    out = nc.dram_tensor("out_dram", inputs["x"].shape, F32, kind="ExternalOutput").ap()
    adaln_ffn(nc, *args, out)
    r = _run(nc, [arrays], core_ids=[0])
    return r.results[0]["out_dram"]
```

```python
from contextlib import ExitStack

import concourse.bass as bass
from concourse import mybir

P = 128
F32 = mybir.dt.float32
F32R = mybir.dt.float32r
U32 = mybir.dt.uint32
I32 = mybir.dt.int32
ALU = mybir.AluOpType
ACT = mybir.ActivationFunctionType



def adaln_ffn(nc, x, lang_ids, slot_ids, W0, Wr0, A0c, B0, route_w, A0f, Bw, W1, b1, lora_As, lora_Bs,
              Wb, b_base, W_router, A1, B1, out):
    NB, SEQ, D = x.shape
    T = NB * SEQ
    NT = T // P
    TPB = SEQ // P
    K = D // P
    E, R, _ = A0c.shape
    ER = E * R
    RC = E + ER
    C0C = ER + E + RC
    MC = RC + D
    MW = MC + R
    ZC = R + RC
    HALF = D // 2
    PART = MW // 3
    Y_OF = [(0, PART - ZC), (PART - ZC, PART), (2 * PART - ZC, PART)]
    LANG_BIAS = 5.0
    GROUPS = [(0, 3), (3, 3), (6, 2)]
    assert (NB, K, E, R, TPB, ER) == (8, 8, 8, 16, 2, 128)

    xf = x.rearrange("b s d -> (b s) d")
    outf = out.rearrange("b s d -> (b s) d")
    fe_hi_dram = nc.dram_tensor("fe_hi_dram", (P + 1, MC), F32, kind="Internal").ap()
    fe_lo_dram = nc.dram_tensor("fe_lo_dram", (P + 1, MC), F32, kind="Internal").ap()

    b1_dram = nc.dram_tensor("b1_dram", (P, D), F32, kind="Internal").ap()
    x1_dram = nc.dram_tensor("x1_dram", (P, D), F32, kind="Internal").ap()

    ctx = ExitStack()
    with ctx:
        def sb(name, shape, dt=F32, where=None):
            return (where or ctx).enter_context(nc.sbuf_tensor(name, shape, dt))

        def sem(name):
            return ctx.enter_context(nc.semaphore(name))

        C0hi = sb("C0hi", [P, K, C0C], F32R)
        C0lo = sb("C0lo", [P, K, C0C], F32R)
        BwThi = sb("BwThi", [P, D], F32R)
        BwTlo = sb("BwTlo", [P, D], F32R)
        D0hi = sb("D0hi", [P, RC], F32R)
        D0lo = sb("D0lo", [P, RC], F32R)
        Ebuf = sb("Ebuf", [96, RC], F32R)
        asraw = sb("asraw", [P, K, R])
        ws_hi = [sb(f"ws_hi{i}", [P, D], F32R) for i in range(2)]
        ws_lo = [sb(f"ws_lo{i}", [P, D], F32R) for i in range(2)]
        wraw_late = [sb(f"wraw{i}", [P, D]) for i in (2, 3)]
        ident = sb("ident", [P, P])
        iota = sb("iota", [P, E])
        ids = sb("ids", [1, 2 * NB], I32)
        lang = sb("lang", [P, NB], I32)
        langf = sb("langf", [P, NB])
        bias = sb("bias", [P, NB * E])
        NBIAS = 2 + K
        bsum = sb("bsum", [P, NBIAS])
        bbase = sb("bbase", [NBIAS, P])
        brow = sb("brow", [NBIAS, P])
        brow_hi, brow_lo = sb("brow_hi", [NBIAS, P], F32R), sb("brow_lo", [NBIAS, P], F32R)
        hs = sb("hs", [P, 96], F32R)
        hsT = sb("hsT", [96, P], F32R)
        hg, wh, wz = sb("hg", [P, ER]), sb("wh", [P, ER]), sb("wz", [P, ER])
        hgThi, hgTlo = sb("hgThi", [P, P], F32R), sb("hgTlo", [P, P], F32R)
        whThi, whTlo = sb("whThi", [P, P], F32R), sb("whTlo", [P, P], F32R)
        wzThi, wzTlo = sb("wzThi", [P, P], F32R), sb("wzTlo", [P, P], F32R)

        def gate_tiles(n):
            return dict(lg=sb(f"lg{n}", [P, E]), mx=sb(f"mx{n}", [P, 8]), ix=sb(f"ix{n}", [P, 8], U32),
                        ixf=sb(f"ixf{n}", [P, 2]), ex=sb(f"ex{n}", [P, 1]), den=sb(f"den{n}", [P, 1]),
                        w=sb(f"w{n}", [P, 2]), ga=sb(f"ga{n}", [P, E]), gb=sb(f"gb{n}", [P, E]),
                        g=sb(f"g{n}", [P, E]))
        G0, G1, GT = gate_tiles("c"), gate_tiles("f"), gate_tiles("t")

        with ExitStack() as first:
            wraw = [sb(f"wraw{i}", [P, D], where=first) for i in (0, 1)] + wraw_late
            R0T = sb("R0T", [P, K, 2 * RC], F32R, first)
            R0Thi, R0Tlo = R0T[:, :, 0:RC], R0T[:, :, RC:2 * RC]
            a0f, a0c = sb("a0f", [P, D], where=first), sb("a0c", [P, D], where=first)
            routers = sb("routers", [E, 2, D], where=first)
            b0raw, bwraw = sb("b0raw", [P, D], where=first), sb("bwraw", [P, D], where=first)
            bw_j, b1_j = sb("bw_j", [P, D], where=first), sb("b1_j", [P, D], where=first)
            b0hi, b0lo = sb("b0hi", [P, D], F32R, first), sb("b0lo", [P, D], F32R, first)
            b_all, b_times = bwraw, a0f
            xin_first, x1_first = sb("xin_first", [P, D], where=first), sb("x1_first", [P, D], where=first)
            xT_first = [sb("xThi_first", [P, D], F32R, first), sb("xTlo_first", [P, D], F32R, first)]
        Mhi = sb("Mhi", [P, K, MW], F32R)
        Mlo = sb("Mlo", [P, K, MW], F32R)

        with ExitStack() as second:
            WbThi, WbTlo = sb("WbThi", [P, K, MC], F32R, second), sb("WbTlo", [P, K, MC], F32R, second)
        B1Thi, B1Tlo = sb("B1Thi", [P, D], F32R), sb("B1Tlo", [P, D], F32R)
        x1 = [sb(f"x1_{i}", [P, D]) for i in range(2)]
        xin = [sb(f"xin{i}", [P, D]) for i in range(2)]
        xT_main = [sb("xThi", [P, D], F32R), sb("xTlo", [P, D], F32R)]
        x1T = [[sb(f"x1Thi{i}", [P, D], F32R), sb(f"x1Tlo{i}", [P, D], F32R)] for i in range(2)]
        ybuf = sb("ybuf", [P, D])
        Fbuf = sb("Fbuf", [96, D], F32R)

        banks = ctx.enter_context(nc.psum_tensor("banks", [P, 8, 512], F32))
        pm = [banks[:, i, :] for i in range(3)]
        p0, pt = banks[:, 3, :], banks[:, 4, :]
        big = [banks[:, 5 + i, :] for i in range(3)]
        pt_h1, pt_hg, pt_wz, pt_wh = (pt[:, P * i:P * (i + 1)] for i in range(4))

        ident_ready = sem("ident_ready")
        gp_step = sem("gp_step")
        memsets_done = sem("memsets_done")
        bias_step = sem("bias_step")
        ids_in, lang_in, b_all_in, bbase_in = sem("ids_in"), sem("lang_in"), sem("b_all_in"), sem("bbase_in")
        a0f_in, a0c_in, routers_in = sem("a0f_in"), sem("a0c_in"), sem("routers_in")
        b0_in, bw_in, b1_in = sem("b0_in"), sem("bw_in"), sem("b1_in")
        bw_j_ready, b1_j_ready, b1_stored = sem("bw_j_ready"), sem("b1_j_ready"), sem("b1_stored")
        x1_stored, x1_back = sem("x1_stored"), sem("x1_back")
        x0_in = sem("x0_in")
        wraw_in = [sem(f"wraw_in{i}") for i in range(4)]
        unit_done, unit_hi, unit_lo = sem("unit_done"), sem("unit_hi"), sem("unit_lo")
        w0_hi, w0_lo, w0_used = sem("w0_hi"), sem("w0_lo"), sem("w0_used")
        b0_hi, b0_lo = sem("b0_hi"), sem("b0_lo")
        c0_half, c0_sum, c0_hi, c0_lo = sem("c0_half"), sem("c0_sum"), sem("c0_hi"), sem("c0_lo")
        d0w_done, d0w_hi, d0w_lo = sem("d0w_done"), sem("d0w_hi"), sem("d0w_lo")
        fe_done, fe_hi, fe_lo, fe_stored = sem("fe_done"), sem("fe_hi"), sem("fe_lo"), sem("fe_stored")
        bsum_step, brow_turned, brow_ready = sem("bsum_step"), sem("brow_turned"), sem("brow_ready")
        brow_split = sem("brow_split")
        w1_hi, w1_lo = sem("w1_hi"), sem("w1_lo")
        m_done, m_hi, m_lo = sem("m_done"), sem("m_hi"), sem("m_lo")
        x_in = [sem(f"x_in{i}") for i in range(2)]
        e_in, f_in, as_in = sem("e_in"), sem("f_in"), sem("as_in")
        as_hi, as_lo = sem("as_hi"), sem("as_lo")
        tx_done, xT_hi, xT_lo = sem("tx_done"), sem("xT_hi"), sem("xT_lo")
        p0_done, h1_done = sem("p0_done"), sem("h1_done")
        g0_step, g1_step, top_step = sem("g0_step"), sem("g1_step"), sem("top_step")
        lg0_ready, lg1_ready, lgt_ready, maxt_ready = (sem(n) for n in ("lg0_ready", "lg1_ready", "lgt_ready", "maxt_ready"))
        max0_ready, max1_ready = sem("max0_ready"), sem("max1_ready")
        exp0_ready, exp1_ready = sem("exp0_ready"), sem("exp1_ready")
        hg_ready, thg_done, hgT_hi, hgT_lo = sem("hg_ready"), sem("thg_done"), sem("hgT_hi"), sem("hgT_lo")
        z0_done, wh_ready, twh_done = sem("z0_done"), sem("wh_ready"), sem("twh_done")
        whT_hi, whT_lo = sem("whT_hi"), sem("whT_lo")
        xl_done, x1_ready, tx1_done = sem("xl_done"), sem("x1_ready"), sem("tx1_done")
        x1T_hi, x1T_lo = sem("x1T_hi"), sem("x1T_lo")
        hs_hi, hs_ready, ths_done, hsT_ready = sem("hs_hi"), sem("hs_ready"), sem("ths_done"), sem("hsT_ready")
        z1_done, wz_ready, twz_done = sem("z1_done"), sem("wz_ready"), sem("twz_done")
        wzT_hi, wzT_lo = sem("wzT_hi"), sem("wzT_lo")
        main_done, y_ready = sem("main_done"), sem("y_ready")
        y_out = sem("y_out")

        block = ctx.enter_context(nc.Block())

        def rows(t, k):
            return t[:, k * P:(k + 1) * P]

        def turn_rc(a, router, thi, tlo, c0, split, waits, router_first):
            units = []
            for k0, n in GROUPS:
                moves = []
                for j in range(n):
                    ao, ro = (j * RC + E, j * RC) if router_first else (j * RC, j * RC + ER)
                    moves += [(ao, ER, split(a, k0 + j)), (ro, E, split(router, k0 + j))]
                dst = [t[:, k0:k0 + n, c0:c0 + RC] for t in (thi, tlo)]
                units.append((moves, dst, (n * RC, "p (k c) -> p k c", dict(k=n)), 1.0, waits))
            return units

        def strided(t, j):
            return t[:, j::K]

        def by_j(t):
            return t[:, :].rearrange("p (e j r) -> p j e r", e=E, j=K)

        def j_first(t):
            return t[:, :].rearrange("p (j e r) -> p j e r", e=E, j=K)

        def turn_b(src, thi, tlo, scale, waits):
            return [([(i * P, P, rows(src, j0 + i)) for i in range(4)],
                     [t[:, :].rearrange("p (o j) -> p o j", j=K)[:, :, j0:j0 + 4] for t in (thi, tlo)],
                     (512, "p (j o) -> p o j", dict(j=4)), scale, waits) for j0 in (0, 4)]

        units_r0 = turn_rc(a0f, routers[:, 1, :], R0Thi, R0Tlo, 0, strided, [(a0f_in, 16), (routers_in, 32)], True)
        units_a0 = turn_rc(a0c, routers[:, 0, :], C0hi, C0lo, 0, rows, [(a0c_in, 16)], False)
        units_bw = turn_b(bw_j, BwThi, BwTlo, 1.0, [(bw_j_ready, 1)])
        units_b1 = turn_b(wraw[2], B1Thi, B1Tlo, 2.0, [(wraw_in[2], 16 * 10)])
        units_wb = []
        for o in range(K):
            for k0 in (0, 4):
                units_wb.append(([(i * P, P, rows(wraw[o % 4], k0 + i)) for i in range(4)],
                                 [t[:, k0:k0 + 4, RC + o * P:RC + (o + 1) * P] for t in (WbThi, WbTlo)],
                                 (512, "p (k c) -> p k c", dict(k=4)), 1.0,
                                 [(wraw_in[o % 4], 16 * (3 + o // 4))]))
        units_r1 = turn_rc(wraw[0], wraw[2][0:E, :], WbThi, WbTlo, 0, rows, [(wraw_in[0], 80), (wraw_in[2], 80)], True)
        units_bs = [([(i * P, P, rows(wraw[1], k0 + i)) for i in range(4)],
                     [t[:, k0 * P:(k0 + 4) * P] for t in (ws_hi[1], ws_lo[1])],
                     (512, None, {}), 1.0, [(wraw_in[1], 16 * (4 + NB))]) for k0 in (0, 4)]
        units_first = units_r0 + units_a0 + units_bw
        units_second = units_wb + units_r1 + units_bs
        NU1 = len(units_first)
        NU2 = NU1 + len(units_second)
        FE_STORES = 2 + 2 * 3

        def psum_of(q, unit):
            width, how, dims = unit[2]
            v = big[q % 3][:, 0:width]
            return v.rearrange(how, **dims) if how else v

        def split_of(hi, lo, k):
            return rows(hi, k), rows(lo, k)

        CHUNKS = [(0, 388), (388, 388), (776, MC - 776)]

        M_BANKS = [pm, big]
        c0_sums = [t[:, 0:4 * RC].rearrange("p (k c) -> p k c", k=4) for t in (a0f, x1_first)]
        XT_BANKS, XL_BANKS = big[1:3], big[0:2]
        XT_FIRST, XL_FIRST = pm[0:2], [pm[2], p0]

        def wait_earlier(eng, s, n):
            if not isinstance(n, int) or n > 0:
                eng.wait_ge(s, n)

        @block.sync
        def _(sp):
            sp.dma_start(a0f[:, :], A0f.rearrange("e r d -> (e r) d")).then_inc(a0f_in, 16)
            sp.dma_start(routers[:, 1, :], route_w).then_inc(routers_in, 16)
            sp.dma_start(routers[:, 0, :], Wr0).then_inc(routers_in, 16)
            w0v = W0.rearrange("(p j) i -> p j i", j=K)

            def wb_used(eng, o):
                eng.wait_ge(unit_done, NU1 + 2 * o + 2)
                eng.wait_ge(bsum_step, o + 1)

            def load_b(raw, src, s):
                sp.dma_start(raw[:, :].rearrange("p (e c) -> p e c", e=E),
                             src.rearrange("e (p j) r -> p e (j r)", j=K)).then_inc(s, 16)

            for j in range(K):
                if j >= 4:
                    sp.wait_ge(w0_hi, j - 3)
                    sp.wait_ge(w0_lo, j - 3)
                sp.dma_start(wraw[j % 4][:, :], w0v[:, j, :]).then_inc(wraw_in[j % 4], 16)
                if j == 3:
                    load_b(b0raw, B0, b0_in)
                    sp.dma_start(a0c[:, :], A0c.rearrange("e r d -> (e r) d")).then_inc(a0c_in, 16)
            load_b(bwraw, Bw, bw_in)
            sp.dma_start(xin_first[:, :], xf[0:P, :]).then_inc(x0_in, 16)
            for o in range(K):
                if o < 4:
                    sp.wait_ge(w0_hi, o + 5)
                    sp.wait_ge(w0_lo, o + 5)
                else:
                    wb_used(sp, o - 4)
                sp.dma_start(wraw[o % 4][:, :], Wb[o * P:(o + 1) * P, :]).then_inc(wraw_in[o % 4], 16)
            sp.wait_ge(b0_lo, 1)
            load_b(b0raw, B1, b1_in)
            wb_used(sp, 4)
            sp.dma_start(wraw[0][:, :], A1.rearrange("e r d -> (e r) d")).then_inc(wraw_in[0], 16)
            sp.wait_ge(ids_in, 32)
            wb_used(sp, 5)
            for b in range(NB):
                slot = sp.value_load(ids[0:1, NB + b:NB + b + 1], min_val=0, max_val=lora_Bs.shape[0] - 1)
                sp.dma_start(wraw[1][b * R:(b + 1) * R, :],
                             lora_Bs[bass.ds(slot, 1), :, :].rearrange("s r d -> (s r) d")).then_inc(wraw_in[1], 16)
            wb_used(sp, 6)
            sp.dma_start(wraw[2][0:E, :], W_router).then_inc(wraw_in[2], 16)
            sp.wait_ge(b1_j_ready, 1)
            sp.dma_start(b1_dram, b1_j[:, :]).then_inc(b1_stored, 16)
            sp.wait_ge(x1_ready, 2)
            sp.dma_start(x1_dram, x1_first[:, :]).then_inc(x1_stored, 16)
            w1v = W1.rearrange("(m p) i -> p m i", p=P)
            wb_used(sp, 7)
            sp.wait_ge(unit_done, NU1 + 2 * K + 3)
            sp.wait_ge(bsum_step, NBIAS)
            for par in range(2):
                sp.dma_start(wraw[2 + par][:, :].rearrange("p (m c) -> p m c", m=K),
                             w1v[:, :, par * P:(par + 1) * P]).then_inc(wraw_in[2 + par], 16)
            sp.wait_ge(brow_split, 2)
            for dram, row in ((fe_hi_dram, brow_hi), (fe_lo_dram, brow_lo)):
                sp.dma_start(dram[P:P + 1, 0:E], row[1:2, 0:E].bitcast(F32)).then_inc(fe_stored, 16)
                sp.dma_start(dram[P:P + 1, E:RC], row[0:1, :].bitcast(F32)).then_inc(fe_stored, 16)
                sp.dma_start(dram[P:P + 1, RC:MC].rearrange("a (k p) -> (a k) p", k=K),
                             row[2:NBIAS, :].bitcast(F32)).then_inc(fe_stored, 16)
            sp.wait_ge(fe_hi, 3)
            sp.wait_ge(fe_lo, 3)
            sp.dma_start(fe_hi_dram[0:P, :], Mhi[:, K - 1, R:MW].bitcast(F32)).then_inc(fe_stored, 16)
            sp.dma_start(fe_lo_dram[0:P, :], Mlo[:, K - 1, R:MW].bitcast(F32)).then_inc(fe_stored, 16)
            with sp.Fori(0, K // 2 - 1) as i:
                for par in range(2):
                    sp.wait_ge(w1_hi, i * 2 + par + 1)
                    sp.wait_ge(w1_lo, i * 2 + par + 1)
                    sp.dma_start(wraw[2 + par][:, :].rearrange("p (m c) -> p m c", m=K),
                                 w1v[:, :, bass.ds((i * 2 + 2 + par) * P, P)]).then_inc(wraw_in[2 + par], 16)

            blocks = [(0, fe_hi_dram), (32, fe_lo_dram), (64, fe_hi_dram)]

            def load_e(b):
                for p, src in blocks:
                    sp.dma_start(Ebuf[p:p + R, :].bitcast(F32), src[bass.ds(b * R, R), 0:RC]).then_inc(e_in, 16)

            def load_f(b):
                for p, src in blocks:
                    sp.dma_start(Fbuf[p:p + R, :].bitcast(F32), src[bass.ds(b * R, R), RC:MC]).then_inc(f_in, 16)

            def load_as(b, guard):
                slot = sp.value_load(ids[0:1, bass.ds(NB + b, 1)], min_val=0, max_val=lora_As.shape[0] - 1)
                src = lora_As[bass.ds(slot, 1), :, :].rearrange("s (k p) r -> p (s k) r", p=P)
                if guard:
                    sp.wait_ge(as_hi, b)
                    sp.wait_ge(as_lo, b)
                sp.dma_start(asraw[:, :, :], src).then_inc(as_in, 16)

            def load_x(t, turn):
                sp.dma_start(xin[turn][:, :], xf[bass.ds(t * P, P), :]).then_inc(x_in[turn], 16)

            sp.wait_ge(w1_hi, K - 1)
            sp.wait_ge(w1_lo, K - 1)
            sp.wait_ge(b1_stored, 16)
            sp.dma_start(wraw[2][:, :], b1_dram).then_inc(wraw_in[2], 16)
            sp.wait_ge(w1_hi, K)
            sp.wait_ge(w1_lo, K)
            sp.wait_ge(x1_stored, 16)
            sp.dma_start(wraw[3][:, :], x1_dram).then_inc(wraw_in[3], 16)
            load_as(0, False)
            sp.wait_ge(m_done, 3 * K)
            load_x(1, 1)
            sp.dma_start(x1[0][:, :], x1_dram).then_inc(x1_back, 16)
            sp.wait_ge(fe_stored, FE_STORES * 16)
            sp.wait_ge(memsets_done, 3)
            load_e(0)
            load_f(0)
            for p, src in blocks[0:2]:
                sp.dma_start(Ebuf[p + R:p + R + 1, :].bitcast(F32), src[P:P + 1, 0:RC]).then_inc(e_in, 16)
                sp.dma_start(Fbuf[p + R:p + R + 1, :].bitcast(F32), src[P:P + 1, RC:MC]).then_inc(f_in, 16)

            def slot_dmas(m, par, b, last, more_x):
                if more_x:
                    sp.wait_ge(x1_ready, m * 2 + 2)
                    load_x(m + 2, par)
                if par == 0 and not last:
                    load_as(b + 1, True)
                if par == 1 and not last:
                    sp.wait_ge(z1_done, m + 1)
                    load_e(b + 1)
                if not (last and par == 1):
                    sp.wait_ge(y_ready, m * 3 + 3)
                    sp.dma_start(outf[bass.ds(m * P, P), :], ybuf[:, :]).then_inc(y_out, 16)
                else:
                    for c, (y0, n) in enumerate(Y_OF):
                        sp.wait_ge(y_ready, m * 3 + c + 1)
                        sp.dma_start(outf[m * P:(m + 1) * P, y0:y0 + n], ybuf[:, y0:y0 + n]).then_inc(y_out, 16)
                if par == 1 and not last:
                    load_f(b + 1)

            for par in range(2):
                slot_dmas(par, par, 0, False, True)
            with sp.Fori(1, NB - 1) as i:
                for par in range(2):
                    slot_dmas(i * 2 + par, par, i, False, True)
            for par in range(2):
                slot_dmas(NT - 2 + par, par, NB - 1, True, False)
            sp.wait_ge(y_out, 16 * (NT - 1 + len(Y_OF)))

        @block.gpsimd
        def _(gp):
            gp.memset(ident[:, :], 0.0).then_inc(gp_step, 1)
            gp.wait_ge(gp_step, 1)
            gp.affine_select(out=ident[:, :], in_=ident[:, :], compare_op=ALU.not_equal, fill=1.0,
                             base=0, pattern=[[-1, P]], channel_multiplier=1).then_inc(ident_ready, 1)
            gp.dma_start(ids[0:1, 0:NB], lang_ids.rearrange("(a b) -> a b", a=1)).then_inc(ids_in, 16)
            gp.dma_start(ids[0:1, NB:2 * NB], slot_ids.rearrange("(a b) -> a b", a=1)).then_inc(ids_in, 16)
            gp.dma_start(lang[:, :], lang_ids.rearrange("(a b) -> a b", a=1).broadcast_to([P, NB])).then_inc(lang_in, 16)
            gp.iota(iota[:, :], pattern=[[1, E]], base=0, channel_multiplier=0,
                    allow_small_or_imprecise_dtypes=True).then_inc(gp_step, 1)
            gp.memset(bsum[:, :], 0.0).then_inc(gp_step, 1)
            gp.memset(bbase[:, :], 0.0).then_inc(gp_step, 1)
            gp.wait_ge(gp_step, 4)
            gp.dma_start(bbase[2:NBIAS, :], b_base.rearrange("(k p) -> k p", k=K)).then_inc(bbase_in, 16)
            gp.wait_ge(bw_in, 16)
            gp.tensor_copy(j_first(bw_j), by_j(bwraw)).then_inc(bw_j_ready, 1)
            gp.wait_ge(bw_j_ready, 1)
            gp.dma_start(b_all[:, :], b1.rearrange("(a i) -> a i", a=1).broadcast_to([P, D])).then_inc(b_all_in, 16)
            gp.wait_ge(b1_in, 16)
            gp.tensor_copy(j_first(b1_j), by_j(b0raw)).then_inc(b1_j_ready, 1)

        @block.scalar
        def _(act):
            def copy_units(q0, units):
                for q, unit in enumerate(units, q0):
                    act.wait_ge(unit_done, q + 1)
                    act.activation(unit[1][0], psum_of(q, unit), ACT.Copy, scale=unit[3]).then_inc(unit_hi, 1)

            def hi_half(done, nth, dst, src, ready):
                act.wait_ge(done, nth)
                act.activation(dst, src, ACT.Copy).then_inc(ready, 1)

            copy_units(0, units_r0)
            for j in range(K):
                act.wait_ge(wraw_in[j % 4], 16 * (j // 4 + 1))
                if j >= 2:
                    act.wait_ge(w0_used, j - 1)
                act.activation(ws_hi[j % 2][:, :], wraw[j % 4][:, :], ACT.Copy).then_inc(w0_hi, 1)
                if j == 5:
                    act.wait_ge(b0_in, 16)
                    act.activation(j_first(b0hi), by_j(b0raw), ACT.Copy).then_inc(b0_hi, 1)
            act.wait_ge(w0_used, K)
            for g in range(2):
                act.activation(c0_sums[g], banks[:, 4 * g:4 * g + 4, RC:2 * RC], ACT.Copy).then_inc(c0_half, 1)
            for g in range(2):
                act.wait_ge(c0_sum, g + 1)
                act.activation(C0hi[:, 4 * g:4 * g + 4, ER + E:C0C], c0_sums[g], ACT.Copy).then_inc(c0_hi, 1)
            act.wait_ge(d0w_done, 1)
            act.activation(D0hi[:, :], p0[:, 0:RC], ACT.Copy, scale=2.0).then_inc(d0w_hi, 1)

            copy_units(3, units_a0 + units_bw)

            def xT_part(t, xT, at=XT_BANKS):
                wait_earlier(act, p0_done, t)
                for h in range(2):
                    hi_half(tx_done, t * 2 + h + 1, xT[0][:, h * HALF:(h + 1) * HALF], at[h][:, :], xT_hi)

            def exp0(t):
                act.wait_ge(max0_ready, t + 1)
                act.activation(G0["ex"][:, :], G0["mx"][:, 0:1], ACT.Exp, bias=G0["mx"][:, 1:2], scale=-1.0)\
                   .then_inc(exp0_ready, 1)

            def exp1(t):
                act.wait_ge(max1_ready, t + 1)
                act.activation(G1["ex"][:, :], G1["mx"][:, 0:1], ACT.Exp, bias=G1["mx"][:, 1:2], scale=-1.0)\
                   .then_inc(exp1_ready, 1)

            def hgT_part(t):
                wait_earlier(act, z0_done, t)
                hi_half(thg_done, t + 1, hgThi[:, :], pt_hg, hgT_hi)

            def whT_part(t):
                wait_earlier(act, xl_done, t * 2)
                hi_half(twh_done, t + 1, whThi[:, :], pt_wh, whT_hi)

            def x1T_part(t, turn):
                wait_earlier(act, main_done, t * 3 - 3)
                for h in range(2):
                    hi_half(tx1_done, t * 2 + h + 1, x1T[turn][0][:, h * HALF:(h + 1) * HALF],
                            big[2 - 2 * h][:, :], x1T_hi)

            def hsT_part(t):
                wait_earlier(act, main_done, t * 3)
                hi_half(ths_done, t + 1, hsT[:, :], pt_h1[0:96, :], hsT_ready)

            def wzT_part(t):
                wait_earlier(act, main_done, t * 3)
                hi_half(twz_done, t + 1, wzThi[:, :], pt_wz, wzT_hi)

            def as_part(b):
                act.wait_ge(as_in, b * 16 + 16)
                wait_earlier(act, h1_done, b * 2)
                act.activation(Mhi[:, :, 0:R], asraw[:, :, :], ACT.Copy).then_inc(as_hi, 1)

            def wb_tiles(o0, o1):
                copy_units(NU1 + 2 * o0, units_wb[2 * o0:2 * o1])

            xT_part(0, xT_first, XT_FIRST)
            wb_tiles(0, 1)
            exp0(0)
            wb_tiles(1, 3)
            hgT_part(0)
            wb_tiles(3, 6)
            whT_part(0)
            wb_tiles(6, K)
            copy_units(NU1 + 2 * K, units_r1 + units_bs)
            act.wait_ge(brow_ready, 1)
            act.activation(brow_hi[:, :], brow[:, :], ACT.Copy).then_inc(brow_split, 1)
            act.wait_ge(wraw_in[2], 96)
            act.activation(ws_hi[0][:, :], wraw[2][:, :], ACT.Copy).then_inc(w1_hi, 1)
            act.wait_ge(x1_stored, 16)
            for c, (c0, n) in enumerate(CHUNKS):
                act.wait_ge(fe_done, c + 1)
                act.activation(Mhi[:, K - 1, R + c0:R + c0 + n], pm[c][:, 0:n], ACT.Copy, scale=2.0).then_inc(fe_hi, 1)
            act.wait_ge(wraw_in[3], 80)
            act.activation(ws_hi[1][:, :], wraw[3][:, :], ACT.Copy).then_inc(w1_hi, 1)
            act.wait_ge(fe_stored, FE_STORES * 16)

            def keep_m(i, par):
                for c, (c0, n) in enumerate(CHUNKS):
                    act.wait_ge(m_done, i * 6 + par * 3 + c + 1)
                    act.activation(Mhi[:, bass.ds(i * 2 + par, 1), R + c0:R + c0 + n],
                                   M_BANKS[par][c][:, 0:n].unsqueeze(1), ACT.Copy).then_inc(m_hi, 1)

            with act.Fori(0, K // 2 - 1) as i:
                for par in range(2):
                    keep_m(i, par)
                    act.wait_ge(wraw_in[2 + par], i * 16 + 16 * (7 - par))
                    act.activation(ws_hi[par][:, :], wraw[2 + par][:, :], ACT.Copy).then_inc(w1_hi, 1)
            for par in range(2):
                keep_m(K // 2 - 1, par)

            copy_units(NU2, units_b1)
            as_part(0)
            x1T_part(0, 0)
            xT_part(1, xT_main)

            def slot(m, par, b, has_a, has_n):
                if has_a:
                    exp0(m + 1)
                    hgT_part(m + 1)
                hsT_part(m)
                exp1(m)
                if has_a:
                    whT_part(m + 1)
                wzT_part(m)
                if has_a:
                    x1T_part(m + 1, 1 - par)
                if has_n:
                    xT_part(m + 2, xT_main)
                if par == 1 and has_n:
                    as_part(b + 1)
            for par in range(2):
                slot(par, par, 0, True, True)
            with act.Fori(1, NB - 1) as i:
                for par in range(2):
                    slot(i * 2 + par, par, i, True, True)
            slot(NT - 2, 0, NB - 1, True, False)
            slot(NT - 1, 1, NB - 1, False, False)

        @block.vector
        def _(dve):
            def lo(out_, src, hi, scale=1.0):
                return dve.scalar_tensor_tensor(out=out_, in0=src, scalar=scale, in1=hi.bitcast(F32),
                                                op0=ALU.mult, op1=ALU.subtract)

            def lo_units(q0, units):
                for q, unit in enumerate(units, q0):
                    dve.wait_ge(unit_hi, q + 1)
                    lo(unit[1][1], psum_of(q, unit), unit[1][0], unit[3]).then_inc(unit_lo, 1)

            dve.memset(hs[:, :].bitcast(F32), 0.0).then_inc(bias_step, 1)
            dve.memset(Ebuf[:, :].bitcast(F32), 0.0).then_inc(memsets_done, 1)
            dve.wait_ge(bias_step, 1)
            dve.memset(hs[:, R:R + 1].bitcast(F32), 1.0).then_inc(memsets_done, 1)
            dve.memset(hs[:, 32 + R:32 + R + 1].bitcast(F32), 1.0).then_inc(bias_step, 1)
            lo_units(0, units_r0)
            for j in range(K):
                dve.wait_ge(w0_hi, j + 1)
                if j >= 2:
                    dve.wait_ge(w0_used, j - 1)
                lo(ws_lo[j % 2][:, :], wraw[j % 4][:, :], ws_hi[j % 2][:, :]).then_inc(w0_lo, 1)
                if j == 5:
                    dve.wait_ge(b0_hi, 1)
                    for j in range(K):
                        ins = lo(j_first(b0lo)[:, j], by_j(b0raw)[:, j], j_first(b0hi)[:, j])
                    ins.then_inc(b0_lo, 1)
            dve.wait_ge(lang_in, 16)
            dve.tensor_copy(langf[:, :], lang[:, :]).then_inc(bias_step, 1)
            dve.wait_ge(bias_step, 3)
            dve.wait_ge(gp_step, 2)
            for b in range(NB):
                dve.tensor_scalar(bias[:, b * E:(b + 1) * E], iota[:, :], langf[:, b:b + 1], LANG_BIAS,
                                  ALU.is_equal, ALU.mult).then_inc(bias_step, 1)
            for g in range(2):
                dve.wait_ge(c0_half, g + 1)
                dve.tensor_tensor(c0_sums[g], banks[:, 4 * g:4 * g + 4, 0:RC], c0_sums[g], ALU.add).then_inc(c0_sum, 1)
            for g in range(2):
                dve.wait_ge(c0_hi, g + 1)
                lo(C0lo[:, 4 * g:4 * g + 4, ER + E:C0C], c0_sums[g], C0hi[:, 4 * g:4 * g + 4, ER + E:C0C])\
                    .then_inc(c0_lo, 1)
            dve.wait_ge(d0w_hi, 1)
            lo(D0lo[:, :], p0[:, 0:RC], D0hi[:, :], 2.0).then_inc(d0w_lo, 1)
            lo_units(3, units_a0 + units_bw)

            def xT_part(t, xT, at=XT_BANKS):
                for h in range(2):
                    dve.wait_ge(xT_hi, t * 2 + h + 1)
                    s = slice(h * HALF, (h + 1) * HALF)
                    lo(xT[1][:, s], at[h][:, :], xT[0][:, s]).then_inc(xT_lo, 1)

            G_STEPS = 8

            def iota_there():
                dve.wait_ge(gp_step, 2)

            def spread(out_, h, g):
                return dve.tensor_tensor(out_.rearrange("p (e r) -> p e r", e=E), h.rearrange("p (e r) -> p e r", e=E),
                                         g[:, :].unsqueeze(2).broadcast_to([P, E, R]), ALU.mult)

            def gates0(t, b):
                dve.wait_ge(p0_done, t + 1)
                dve.tensor_tensor(G0["lg"][:, :], p0[:, ER:ER + E], bias[:, bass.ds(b * E, E)], ALU.add).then_inc(lg0_ready, 1)
                iota_there()
                dve.wait_ge(lg0_ready, t + 1)
                gates_from(G0, G0["lg"][:, :], t, g0_step, max0_ready, exp0_ready)
                wait_earlier(dve, thg_done, t)
                spread(hg[:, :], p0[:, 0:ER], G0["g"]).then_inc(hg_ready, 1)

            def gates_from(G, logits, t, step, max_ready, exp_ready, meanwhile=None):
                def at(n):
                    dve.wait_ge(step, t * G_STEPS + n)
                dve.max(G["mx"][:, :], logits).then_inc(max_ready, 1)
                iota_there()
                dve.wait_ge(max_ready, t + 1)
                dve.max_index(G["ix"][:, :], G["mx"][:, :], logits).then_inc(step, 1)
                at(1)
                dve.tensor_copy(G["ixf"][:, :], G["ix"][:, 0:2]).then_inc(step, 1)
                if meanwhile:
                    meanwhile()
                dve.wait_ge(exp_ready, t + 1)
                dve.tensor_scalar(G["den"][:, :], G["ex"][:, :], 1.0, None, ALU.add).then_inc(step, 1)
                at(3)
                dve.reciprocal(G["w"][:, 0:1], G["den"][:, :]).then_inc(step, 1)
                at(4)
                dve.tensor_tensor(G["w"][:, 1:2], G["ex"][:, :], G["w"][:, 0:1], ALU.mult).then_inc(step, 1)
                dve.tensor_scalar(G["ga"][:, :], iota[:, :], G["ixf"][:, 0:1], G["w"][:, 0:1],
                                  ALU.is_equal, ALU.mult).then_inc(step, 1)
                at(5)
                dve.tensor_scalar(G["gb"][:, :], iota[:, :], G["ixf"][:, 1:2], G["w"][:, 1:2],
                                  ALU.is_equal, ALU.mult).then_inc(step, 1)
                at(7)
                dve.tensor_tensor(G["g"][:, :], G["ga"][:, :], G["gb"][:, :], ALU.add).then_inc(step, 1)
                at(8)

            def gates1(t, meanwhile):
                dve.wait_ge(z1_done, t + 1)
                dve.tensor_copy(G1["lg"][:, :], pm[0][:, R:R + E]).then_inc(lg1_ready, 1)
                iota_there()
                dve.wait_ge(lg1_ready, t + 1)
                gates_from(G1, G1["lg"][:, :], t, g1_step, max1_ready, exp1_ready, meanwhile)
                wait_earlier(dve, twz_done, t)
                spread(wz[:, :], pm[0][:, R + E:ZC], G1["g"]).then_inc(wz_ready, 1)

            def top1(t):
                TOP = 3

                def at(n):
                    dve.wait_ge(top_step, t * TOP + n)
                z = ER + E
                dve.wait_ge(z0_done, t + 1)
                dve.tensor_copy(GT["lg"][:, :], p0[:, z:z + E]).then_inc(lgt_ready, 1)
                iota_there()
                dve.wait_ge(lgt_ready, t + 1)
                dve.max(GT["mx"][:, :], GT["lg"][:, :]).then_inc(maxt_ready, 1)
                iota_there()
                dve.wait_ge(maxt_ready, t + 1)
                dve.max_index(GT["ix"][:, :], GT["mx"][:, :], GT["lg"][:, :]).then_inc(top_step, 1)
                at(1)
                dve.tensor_copy(GT["ixf"][:, :], GT["ix"][:, 0:2]).then_inc(top_step, 1)
                at(2)
                dve.tensor_scalar(GT["g"][:, :], iota[:, :], GT["ixf"][:, 0:1], GT["mx"][:, 0:1],
                                  ALU.is_equal, ALU.mult).then_inc(top_step, 1)
                at(3)
                wait_earlier(dve, twh_done, t)
                spread(wh[:, :], p0[:, z + E:C0C], GT["g"]).then_inc(wh_ready, 1)

            def hgT_part(t):
                dve.wait_ge(hgT_hi, t + 1)
                lo(hgTlo[:, :], pt_hg, hgThi[:, :]).then_inc(hgT_lo, 1)

            def whT_part(t):
                dve.wait_ge(whT_hi, t + 1)
                lo(whTlo[:, :], pt_wh, whThi[:, :]).then_inc(whT_lo, 1)

            def wzT_part(t):
                dve.wait_ge(wzT_hi, t + 1)
                lo(wzTlo[:, :], pt_wz, wzThi[:, :]).then_inc(wzT_lo, 1)

            def x1_part(t, dst, src, at=XL_BANKS):
                wait_earlier(dve, tx1_done, t * 2 - 2)
                for h in range(2):
                    dve.wait_ge(xl_done, t * 2 + h + 1)
                    s = slice(h * HALF, (h + 1) * HALF)
                    dve.tensor_tensor(dst[:, s], at[h][:, :], src[:, s], ALU.add).then_inc(x1_ready, 1)

            def x1T_part(t, turn):
                for h in range(2):
                    dve.wait_ge(x1T_hi, t * 2 + h + 1)
                    s = slice(h * HALF, (h + 1) * HALF)
                    lo(x1T[turn][1][:, s], big[2 - 2 * h][:, :], x1T[turn][0][:, s]).then_inc(x1T_lo, 1)

            def hs_part(t):
                dve.wait_ge(h1_done, t + 1)
                wait_earlier(dve, ths_done, t)
                dve.tensor_copy(hs[:, 0:64].rearrange("p (b c) -> p b c", b=2)[:, :, 0:R],
                                pm[0][:, 0:R].unsqueeze(1).broadcast_to([P, 2, R])).then_inc(hs_hi, 1)
                dve.wait_ge(hs_hi, t + 1)
                lo(hs[:, 64:64 + R], pm[0][:, 0:R], hs[:, 0:R]).then_inc(hs_ready, 1)

            def y_part(t, turn, c):
                y0, n = Y_OF[c]
                dve.wait_ge(main_done, t * 3 + c + 1)
                if c == 0:
                    wait_earlier(dve, y_out, t * 16)
                dve.tensor_tensor(ybuf[:, y0:y0 + n], pm[c][:, PART - n:PART], x1[turn][:, y0:y0 + n], ALU.add)\
                   .then_inc(y_ready, 1)

            def as_part(b):
                dve.wait_ge(as_hi, b + 1)
                lo(Mlo[:, :, 0:R], asraw[:, :, :], Mhi[:, :, 0:R]).then_inc(as_lo, 1)

            def b_sum(nth, col, src):
                if nth > 0:
                    dve.wait_ge(bsum_step, nth)
                n = src.shape[0]
                dve.tensor_tensor_reduce(out=b_times[0:n, :], in0=src, in1=b_all[0:n, :], scale=1.0, scalar=0.0,
                                         op0=ALU.mult, op1=ALU.add, accum_out=bsum[0:n, col:col + 1])\
                   .then_inc(bsum_step, 1)

            def wb_tiles(o0, o1):
                for o in range(o0, o1):
                    lo_units(NU1 + 2 * o, units_wb[2 * o:2 * o + 2])
                    b_sum(o, 2 + o, wraw[o % 4][:, :])

            dve.wait_ge(bias_step, 3 + NB)
            xT_part(0, xT_first, XT_FIRST)
            dve.wait_ge(b_all_in, 16)
            dve.wait_ge(gp_step, 4)
            wb_tiles(0, 1)
            gates0(0, 0)
            wb_tiles(1, 3)
            hgT_part(0)
            wb_tiles(3, 4)
            top1(0)
            wb_tiles(4, 6)
            whT_part(0)
            wb_tiles(6, 7)
            x1_part(0, x1_first, xin_first, XL_FIRST)
            wb_tiles(7, K)
            lo_units(NU1 + 2 * K, units_r1[0:3])
            b_sum(K, 0, wraw[0][:, :])
            b_sum(K + 1, 1, wraw[2][0:E, :])
            lo_units(NU1 + 2 * K + 3, units_bs)
            dve.wait_ge(bbase_in, 16)
            dve.wait_ge(brow_turned, 1)
            dve.tensor_tensor(brow[:, :], pt[0:NBIAS, 0:P], bbase[:, :], ALU.add).then_inc(brow_ready, 1)
            dve.wait_ge(brow_split, 1)
            lo(brow_lo[:, :], brow[:, :], brow_hi[:, :]).then_inc(brow_split, 1)
            dve.wait_ge(w1_hi, 1)
            lo(ws_lo[0][:, :], wraw[2][:, :], ws_hi[0][:, :]).then_inc(w1_lo, 1)
            for c, (c0, n) in enumerate(CHUNKS):
                dve.wait_ge(fe_hi, c + 1)
                lo(Mlo[:, K - 1, R + c0:R + c0 + n], pm[c][:, 0:n], Mhi[:, K - 1, R + c0:R + c0 + n], 2.0)\
                    .then_inc(fe_lo, 1)
            dve.wait_ge(w1_hi, 2)
            lo(ws_lo[1][:, :], wraw[3][:, :], ws_hi[1][:, :]).then_inc(w1_lo, 1)
            dve.wait_ge(fe_stored, FE_STORES * 16)

            def keep_m(i, par):
                for c, (c0, n) in enumerate(CHUNKS):
                    dve.wait_ge(m_hi, i * 6 + par * 3 + c + 1)
                    lo(Mlo[:, bass.ds(i * 2 + par, 1), R + c0:R + c0 + n], M_BANKS[par][c][:, 0:n].unsqueeze(1),
                       Mhi[:, bass.ds(i * 2 + par, 1), R + c0:R + c0 + n]).then_inc(m_lo, 1)

            with dve.Fori(0, K // 2 - 1) as i:
                for par in range(2):
                    keep_m(i, par)
                    dve.wait_ge(w1_hi, i * 2 + 3 + par)
                    lo(ws_lo[par][:, :], wraw[2 + par][:, :], ws_hi[par][:, :]).then_inc(w1_lo, 1)
            for par in range(2):
                keep_m(K // 2 - 1, par)

            dve.wait_ge(m_done, 3 * K)
            dve.memset(Fbuf[:, :].bitcast(F32), 0.0).then_inc(memsets_done, 1)
            lo_units(NU2, units_b1)
            as_part(0)
            x1T_part(0, 0)
            xT_part(1, xT_main)
            dve.wait_ge(x1_back, 16)

            def slot(m, par, b, has_a, has_n):
                if has_a:
                    gates0(m + 1, b + par)
                    hgT_part(m + 1)
                hs_part(m)
                if has_a:
                    top1(m + 1)
                gates1(m, (lambda: whT_part(m + 1)) if has_a else None)
                if has_a:
                    x1_part(m + 1, x1[1 - par], xin[1 - par])
                wzT_part(m)
                if has_a:
                    x1T_part(m + 1, 1 - par)
                y_part(m, par, 0)
                y_part(m, par, 1)
                if has_n:
                    xT_part(m + 2, xT_main)
                if par == 1 and has_n:
                    as_part(b + 1)
                y_part(m, par, 2)
            for par in range(2):
                slot(par, par, 0, True, True)
            with dve.Fori(1, NB - 1) as i:
                for par in range(2):
                    slot(i * 2 + par, par, i, True, True)
            slot(NT - 2, 0, NB - 1, True, False)
            slot(NT - 1, 1, NB - 1, False, False)

        @block.tensor
        def _(pe):
            def turn_units(q0, units):
                for q, unit in enumerate(units, q0):
                    for s, v in unit[4]:
                        pe.wait_ge(s, v)
                    if q >= 3:
                        pe.wait_ge(unit_lo, q - 2)
                    moves = unit[0]
                    for n, (col, width, src) in enumerate(moves):
                        kp = src.shape[0]
                        ins = pe.transpose(big[q % 3][:, col:col + width], src, ident[0:kp, 0:kp])
                    ins.then_inc(unit_done, 1)

            def three(out_, l, r, start, stop, **kw):
                pe.matmul(out_, l[0], r[0], start=start, stop=False, **kw)
                pe.matmul(out_, l[0], r[1], start=False, stop=False, **kw)
                return pe.matmul(out_, l[1], r[0], start=False, stop=stop, **kw)

            pe.wait_ge(ident_ready, 1)
            turn_units(0, units_r0)
            pe.wait_ge(unit_lo, 3)
            for j in range(K):
                pe.wait_ge(w0_lo, j + 1)
                for k in range(K):
                    for n, w in enumerate(split_of(ws_hi[j % 2], ws_lo[j % 2], k)):
                        ins = pe.matmul(banks[:, k, 0:2 * RC], w, R0T[:, j, :], start=j == 0 and n == 0,
                                        stop=j == K - 1 and n == 1)
                ins.then_inc(w0_used, 1)
            pe.wait_ge(b0_lo, 1)
            pe.wait_ge(c0_sum, 1)
            for j in range(K):
                ins = three(p0[:, 0:RC], split_of(b0hi, b0lo, j), (R0Thi[:, j, :], R0Tlo[:, j, :]),
                            j == 0, j == K - 1)
            ins.then_inc(d0w_done, 1)
            pe.wait_ge(c0_sum, 2)
            turn_units(3, units_a0 + units_bw)

            def turn_x(src, at):
                for h in range(2):
                    for k in range(4):
                        ins = pe.transpose(rows(at[h], k), rows(src, 4 * h + k), ident[:, :])
                    ins.then_inc(tx_done, 1)

            def small0(t, xT):
                pe.wait_ge(xT_lo, t * 2 + 2)
                for k in range(K):
                    ins = three(p0[:, 0:C0C], split_of(xT[0], xT[1], k), (C0hi[:, k, :], C0lo[:, k, :]),
                                k == 0, k == K - 1, skip_group_check=True)
                ins.then_inc(p0_done, 1)

            def turn_small(s, nth, dst, src, done):
                pe.wait_ge(s, nth)
                pe.transpose(dst, src, ident[:, :]).then_inc(done, 1)

            def add_lora0(t):
                pe.wait_ge(hgT_lo, t + 1)
                three(p0[:, ER + E:C0C], (hgThi[:, :], hgTlo[:, :]), (D0hi[:, :], D0lo[:, :]), False, True,
                      skip_group_check=True).then_inc(z0_done, 1)

            def ffn0(t, guard, at=XL_BANKS):
                pe.wait_ge(whT_lo, t + 1)
                for h in range(2):
                    if guard:
                        if h == 0:
                            pe.wait_ge(x1T_lo, t * 2)
                        else:
                            pe.wait_ge(xT_lo, t * 2 + 1)
                    s = slice(h * HALF, (h + 1) * HALF)
                    three(at[h][:, :], (whThi[:, :], whTlo[:, :]), (BwThi[:, s], BwTlo[:, s]), True, True)\
                        .then_inc(xl_done, 1)

            def turn_x1(t, src):
                for h in range(2):
                    if h == 0:
                        pe.wait_ge(xT_lo, t * 2 + 2)
                        pe.wait_ge(x1_ready, t * 2 + 1)
                    else:
                        pe.wait_ge(x1_ready, t * 2 + 2)
                    for k in range(4):
                        ins = pe.transpose(rows(big[2 - 2 * h], k), rows(src, 4 * h + k), ident[:, :])
                    ins.then_inc(tx1_done, 1)

            def turn_x_main(t, turn, nth):
                pe.wait_ge(x_in[turn], nth * 16)
                for h in range(2):
                    if h == 0:
                        pe.wait_ge(x1_ready, t * 2)
                    else:
                        pe.wait_ge(x1T_lo, t * 2 - 1)
                    for k in range(4):
                        ins = pe.transpose(rows(big[1 + h], k), rows(xin[turn], 4 * h + k), ident[:, :])
                    ins.then_inc(tx_done, 1)

            def wb_tiles(o0, o1):
                turn_units(NU1 + 2 * o0, units_wb[2 * o0:2 * o1])

            pe.wait_ge(x0_in, 16)
            turn_x(xin_first, XT_FIRST)
            wb_tiles(0, 1)
            pe.wait_ge(c0_lo, 2)
            pe.wait_ge(d0w_lo, 1)
            small0(0, xT_first)
            wb_tiles(1, 3)
            turn_small(hg_ready, 1, pt_hg, hg[:, :], thg_done)
            wb_tiles(3, 4)
            add_lora0(0)
            wb_tiles(4, 6)
            turn_small(wh_ready, 1, pt_wh, wh[:, :], twh_done)
            wb_tiles(6, 7)
            ffn0(0, False, XL_FIRST)
            wb_tiles(7, K)

            turn_units(NU1 + 2 * K, units_r1 + units_bs)
            pe.wait_ge(bsum_step, NBIAS)
            pe.transpose(pt[0:NBIAS, 0:P], bsum[:, :], ident[:, :]).then_inc(brow_turned, 1)
            pe.wait_ge(unit_lo, NU2)
            pe.wait_ge(x1_ready, 2)
            for c, (c0, n) in enumerate(CHUNKS):
                for k in range(K):
                    ins = three(pm[c][:, 0:n], split_of(ws_hi[1], ws_lo[1], k),
                                (WbThi[:, k, c0:c0 + n], WbTlo[:, k, c0:c0 + n]), k == 0, k == K - 1)
                ins.then_inc(fe_done, 1)

            pe.wait_ge(fe_lo, 3)

            def m_tile(i, par, guard):
                pe.wait_ge(w1_lo, i * 2 + par + 1)
                for c, (c0, n) in enumerate(CHUNKS):
                    if guard:
                        pe.wait_ge(m_lo, i * 6 + par * 3 + c - 5)
                    for k in range(K):
                        ins = three(M_BANKS[par][c][:, 0:n], split_of(ws_hi[par], ws_lo[par], k),
                                    (WbThi[:, k, c0:c0 + n], WbTlo[:, k, c0:c0 + n]), k == 0, k == K - 1)
                    ins.then_inc(m_done, 1)
            for par in range(2):
                m_tile(0, par, False)
            with pe.Fori(1, K // 2) as i:
                for par in range(2):
                    m_tile(i, par, True)

            pe.wait_ge(m_lo, 3 * K)
            pe.wait_ge(memsets_done, 3)
            pe.wait_ge(bias_step, 3)
            turn_units(NU2, units_b1)
            pe.wait_ge(wraw_in[3], 16 * 9)
            pe.wait_ge(unit_lo, NU2 + 2)
            turn_x1(0, wraw[3])
            turn_x_main(1, 1, 1)

            def slot(m, par, b, has_a, has_n):
                a, n = m + 1, m + 2
                xa = x1T[par]

                def main(c, k0, k1):
                    for k in range(k0, k1):
                        s = slice(c * PART, (c + 1) * PART)
                        ins = three(pm[c][:, 0:PART], split_of(xa[0], xa[1], k), (Mhi[:, k, s], Mlo[:, k, s]),
                                    k == 0, c == 0 and k == K - 1, skip_group_check=True)
                    return ins

                def lora(c):
                    y0, n = Y_OF[c]
                    y, s = pm[c][:, PART - n:PART], slice(y0, y0 + n)
                    three(y, (wzThi[:, :], wzTlo[:, :]), (B1Thi[:, s], B1Tlo[:, s]), False, False,
                          skip_group_check=True)
                    pe.matmul(y, hsT[:, :], Fbuf[:, s], start=False, stop=True, skip_group_check=True)\
                      .then_inc(main_done, 1)

                if has_a:
                    small0(a, xT_main)
                else:
                    pe.wait_ge(y_ready, m * 3)
                pe.wait_ge(x1T_lo, m * 2 + 2)
                pe.wait_ge(as_lo, b + 1)
                if has_a:
                    main(0, 0, 7)
                    turn_small(hg_ready, a + 1, pt_hg, hg[:, :], thg_done)
                    main(0, 7, K).then_inc(h1_done, 1)
                    main(1, 0, 1)
                    add_lora0(a)
                    main(1, 1, 2)
                else:
                    main(0, 0, K).then_inc(h1_done, 1)
                    main(1, 0, 2)
                turn_small_hs(m)
                main(1, 2, 4)
                pe.wait_ge(hsT_ready, m + 1)
                pe.wait_ge(e_in, b * 48 + 48 + 32)
                pe.matmul(pm[0][:, R:ZC], hsT[:, :], Ebuf[:, :], start=False, stop=True,
                          skip_group_check=True).then_inc(z1_done, 1)
                main(1, 4, 6)
                if has_a:
                    turn_small(wh_ready, a + 1, pt_wh, wh[:, :], twh_done)
                main(1, 6, K)
                if has_a:
                    ffn0(a, True)
                main(2, 0, 1)
                turn_small(wz_ready, m + 1, pt_wz, wz[:, :], twz_done)
                main(2, 1, 4)
                if has_a:
                    turn_x1(a, x1[1 - par])
                pe.wait_ge(wzT_lo, m + 1)
                pe.wait_ge(f_in, b * 48 + 48 + 32)
                lora(0)
                lora(1)
                main(2, 4, 6)
                if has_n:
                    turn_x_main(n, par, (b + 1) + (1 if par == 1 else 0))
                main(2, 6, K)
                lora(2)

            def turn_small_hs(m):
                pe.wait_ge(hs_ready, m + 1)
                pe.transpose(pt_h1[0:96, :], hs[:, :].bitcast(F32), ident[:, :]).then_inc(ths_done, 1)

            for par in range(2):
                slot(par, par, 0, True, True)
            with pe.Fori(1, NB - 1) as i:
                for par in range(2):
                    slot(i * 2 + par, par, i, True, True)
            slot(NT - 2, 0, NB - 1, True, False)
            slot(NT - 1, 1, NB - 1, False, False)


_INS = ['x', 'itok_B_0_7', 'itok_B_0_23', 'L0_cond_W', 'L0_cond_Wr', 'L0_cond_A', 'L0_cond_B', 'L0_ffn_route_w',
        'L0_ffn_A', 'L0_ffn_Bw', 'L1_cond_W', 'L1_cond_b', 'L1_cond_lora_As', 'L1_cond_lora_Bs', 'L1_ffn_W_base',
        'L1_ffn_b_base', 'L1_ffn_W_router', 'L1_ffn_A', 'L1_ffn_B']


def kernel(**inputs):
    import numpy as _np
    import concourse.bacc as _bacc
    from concourse import mybir as _mybir
    from concourse.bass_utils import run_bass_kernel_spmd as _run

    nc = _bacc.Bacc("TRN2", target_bir_lowering=False, num_devices=1)
    arrays, args = {}, []
    for name in _INS:
        a = _np.ascontiguousarray(inputs[name])
        arrays[f"in_{name}_dram"] = a
        args.append(nc.dram_tensor(f"in_{name}_dram", a.shape, _mybir.dt.from_np(a.dtype), kind="ExternalInput").ap())
    out = nc.dram_tensor("out_dram", inputs["x"].shape, F32, kind="ExternalOutput").ap()
    adaln_ffn(nc, *args, out)
    r = _run(nc, [arrays], core_ids=[0])
    return r.results[0]["out_dram"]
```

```python
from contextlib import ExitStack

import concourse.bass as bass
from concourse import mybir

P = 128
F32 = mybir.dt.float32
F32R = mybir.dt.float32r
U32 = mybir.dt.uint32
I32 = mybir.dt.int32
ALU = mybir.AluOpType
ACT = mybir.ActivationFunctionType



def adaln_ffn(nc, x, lang_ids, slot_ids, W0, Wr0, A0c, B0, route_w, A0f, Bw, W1, b1, lora_As, lora_Bs,
              Wb, b_base, W_router, A1, B1, out):
    NB, SEQ, D = x.shape
    T = NB * SEQ
    NT = T // P
    TPB = SEQ // P
    K = D // P
    E, R, _ = A0c.shape
    ER = E * R
    RC = E + ER
    C0C = ER + E + RC
    MC = RC + D
    MW = MC + R
    ZC = R + RC
    HALF = D // 2
    PART = MW // 3
    Y_OF = [(0, PART - ZC), (PART - ZC, PART), (2 * PART - ZC, PART)]
    LANG_BIAS = 5.0
    GROUPS = [(0, 3), (3, 3), (6, 2)]
    assert (NB, K, E, R, TPB, ER) == (8, 8, 8, 16, 2, 128)

    xf = x.rearrange("b s d -> (b s) d")
    outf = out.rearrange("b s d -> (b s) d")
    fe_hi_dram = nc.dram_tensor("fe_hi_dram", (P + 1, MC), F32, kind="Internal").ap()
    fe_lo_dram = nc.dram_tensor("fe_lo_dram", (P + 1, MC), F32, kind="Internal").ap()

    b1_dram = nc.dram_tensor("b1_dram", (P, D), F32, kind="Internal").ap()
    x1T_dram = nc.dram_tensor("x1T_dram", (P, 2 * D), F32, kind="Internal").ap()

    ctx = ExitStack()
    with ctx:
        def sb(name, shape, dt=F32, where=None):
            return (where or ctx).enter_context(nc.sbuf_tensor(name, shape, dt))

        def sem(name):
            return ctx.enter_context(nc.semaphore(name))

        C0hi = sb("C0hi", [P, K, C0C], F32R)
        C0lo = sb("C0lo", [P, K, C0C], F32R)
        BwThi = sb("BwThi", [P, D], F32R)
        BwTlo = sb("BwTlo", [P, D], F32R)
        D0hi = sb("D0hi", [P, RC], F32R)
        D0lo = sb("D0lo", [P, RC], F32R)
        Ebuf = sb("Ebuf", [96, RC], F32R)
        asraw = sb("asraw", [P, K, R])
        ws_hi = [sb(f"ws_hi{i}", [P, D], F32R) for i in range(2)]
        ws_lo = [sb(f"ws_lo{i}", [P, D], F32R) for i in range(2)]
        wraw_late = [sb(f"wraw{i}", [P, D]) for i in (2, 3)]
        ident = sb("ident", [P, P])
        iota = sb("iota", [P, E])
        ids = sb("ids", [1, 2 * NB], I32)
        lang = sb("lang", [P, NB], I32)
        langf = sb("langf", [P, NB])
        bias = sb("bias", [P, NB * E])
        brow, bcol = sb("brow", [K, P]), sb("bcol", [P, K])
        ones = sb("ones", [P, P])
        hs = sb("hs", [P, 96], F32R)
        hsT = sb("hsT", [96, P], F32R)
        hg, wh, wz = sb("hg", [P, ER]), sb("wh", [P, ER]), sb("wz", [P, ER])
        hgThi, hgTlo = sb("hgThi", [P, P], F32R), sb("hgTlo", [P, P], F32R)
        whThi, whTlo = sb("whThi", [P, 2 * P], F32R), sb("whTlo", [P, 2 * P], F32R)
        wzThi, wzTlo = sb("wzThi", [P, P], F32R), sb("wzTlo", [P, P], F32R)

        def gate_tiles(n):
            return dict(lg=sb(f"lg{n}", [P, E]), mx=sb(f"mx{n}", [P, 8]), ix=sb(f"ix{n}", [P, 8], U32),
                        ixf=sb(f"ixf{n}", [P, 2]), ex=sb(f"ex{n}", [P, 1]), den=sb(f"den{n}", [P, 1]),
                        w=sb(f"w{n}", [P, 2]), ga=sb(f"ga{n}", [P, E]), gb=sb(f"gb{n}", [P, E]),
                        g=sb(f"g{n}", [P, E]))
        G0, G1, GT = gate_tiles("c"), gate_tiles("f"), gate_tiles("t")

        with ExitStack() as first:
            wraw = [sb(f"wraw{i}", [P, D], where=first) for i in (0, 1)] + wraw_late
            xT_first = [sb("xThi_first", [P, 2 * D], F32R, first), sb("xTlo_first", [P, 2 * D], F32R, first)]
            xin_first = sb("xin_first", [P, 2 * D], where=first)
            a0f, a0c = sb("a0f", [P, D], where=first), sb("a0c", [P, D], where=first)
            routers = sb("routers", [E, 2, D], where=first)
            R0T = sb("R0T", [P, K, 2 * RC], F32R, first)
            R0Thi, R0Tlo = R0T[:, :, 0:RC], R0T[:, :, RC:2 * RC]
            bw_j, b1_j = sb("bw_j", [P, D], where=first), sb("b1_j", [P, D], where=first)
            b0raw, bwraw = sb("b0raw", [P, D], where=first), sb("bwraw", [P, D], where=first)
        with ExitStack() as before_m:
            sb("below_b_acc", [P, (K - 1) * MW + R], where=before_m)
            b_acc = sb("b_acc", [P, MC], where=before_m)
            sb("below_x2", [P, (K - 1) * MW + R], where=before_m)
            x2_early = sb("x2_early", [P, D], where=before_m)
        Mhi = sb("Mhi", [P, K, MW], F32R)
        Mlo = sb("Mlo", [P, K, MW], F32R)

        with ExitStack() as zeroth:
            w0s_hi = ws_hi + [sb(f"w0s_hi{i}", [P, D], F32R, zeroth) for i in (2, 3)]
            w0s_lo = ws_lo + [sb(f"w0s_lo{i}", [P, D], F32R, zeroth) for i in (2, 3)]
            b0hi, b0lo = sb("b0hi", [P, D], F32R, zeroth), sb("b0lo", [P, D], F32R, zeroth)
        with ExitStack() as second:
            WbThi, WbTlo = sb("WbThi", [P, K, MC], F32R, second), sb("WbTlo", [P, K, MC], F32R, second)
        B1Thi, B1Tlo = ws_hi[0], ws_lo[0]
        xin = [sb(f"xin{i}", [P, D]) for i in range(2)]
        xT_main = [sb("xThi", [P, 2 * D], F32R), sb("xTlo", [P, 2 * D], F32R)]
        x1T = [[sb(f"x1Thi{i}", [P, 2 * D], F32R), sb(f"x1Tlo{i}", [P, 2 * D], F32R)] for i in range(2)]
        x1_sums = sb("x1_sums", [P, 2 * D])
        ybuf = sb("ybuf", [P, D])
        Fbuf = sb("Fbuf", [96, D], F32R)

        banks = ctx.enter_context(nc.psum_tensor("banks", [P, 8, 512], F32))
        pm = [banks[:, i, :] for i in range(3)]
        p0, pt = banks[:, 3, :], banks[:, 4, :]
        big = [banks[:, 5 + i, :] for i in range(3)]
        pt_h1, pt_hg, pt_wz, pt_wh = (pt[:, P * i:P * (i + 1)] for i in range(4))

        ident_ready = sem("ident_ready")
        gp_step = sem("gp_step")
        memsets_done = sem("memsets_done")
        bias_step = sem("bias_step")
        ids_in, lang_in, brow_in, bbase_in = sem("ids_in"), sem("lang_in"), sem("brow_in"), sem("bbase_in")
        a0f_in, a0c_in, r0_in = sem("a0f_in"), sem("a0c_in"), sem("r0_in")
        b0_in, bw_in, b1_in = sem("b0_in"), sem("bw_in"), sem("b1_in")
        bw_j_ready, b1_j_ready, b1_stored = sem("bw_j_ready"), sem("b1_j_ready"), sem("b1_stored")
        x1_stored = sem("x1_stored")
        wr0_in, a1_in, r1_in, bs_in = (sem(n) for n in ("wr0_in", "a1_in", "r1_in", "bs_in"))
        x0_in = sem("x0_in")
        wraw_in = [sem(f"wraw_in{i}") for i in range(4)]
        unit_done, unit_hi, unit_lo = sem("unit_done"), sem("unit_hi"), sem("unit_lo")
        w0_hi, w0_lo, w0_used = sem("w0_hi"), sem("w0_lo"), sem("w0_used")
        b0_hi, b0_lo = sem("b0_hi"), sem("b0_lo")
        c0_done = sem("c0_done")
        c0_half, c0_sum, c0_hi, c0_lo = sem("c0_half"), sem("c0_sum"), sem("c0_hi"), sem("c0_lo")
        d0w_done, d0w_hi, d0w_lo = sem("d0w_done"), sem("d0w_hi"), sem("d0w_lo")
        fe_done, fe_hi, fe_lo, fe_stored = sem("fe_done"), sem("fe_hi"), sem("fe_lo"), sem("fe_stored")
        bcol_turned, bcol_ready, acc_step = sem("bcol_turned"), sem("bcol_ready"), sem("acc_step")
        bias_done, brow_hi, brow_lo = sem("bias_done"), sem("brow_hi"), sem("brow_lo")
        w1_hi, w1_lo = sem("w1_hi"), sem("w1_lo")
        m_done, m_hi, m_lo = sem("m_done"), sem("m_hi"), sem("m_lo")
        x_in = [sem(f"x_in{i}") for i in range(2)]
        e_in, f_in, as_in = sem("e_in"), sem("f_in"), sem("as_in")
        as_hi, as_lo = sem("as_hi"), sem("as_lo")
        tx_done, xT_hi, xT_lo = sem("tx_done"), sem("xT_hi"), sem("xT_lo")
        p0_done, h1_done = sem("p0_done"), sem("h1_done")
        g0_step, g1_step, top_step = sem("g0_step"), sem("g1_step"), sem("top_step")
        lg0_ready, lg1_ready, lgt_ready = (sem(n) for n in ("lg0_ready", "lg1_ready", "lgt_ready"))
        maxt_ready = sem("maxt_ready")
        max0_ready, max1_ready = sem("max0_ready"), sem("max1_ready")
        exp0_ready, exp1_ready = sem("exp0_ready"), sem("exp1_ready")
        hg_ready, thg_done, hgT_hi, hgT_lo = sem("hg_ready"), sem("thg_done"), sem("hgT_hi"), sem("hgT_lo")
        z0_done, wh_ready, twh_done = sem("z0_done"), sem("wh_ready"), sem("twh_done")
        whT_hi, whT_lo = sem("whT_hi"), sem("whT_lo")
        x1w_done, x1_half, x1_sum = sem("x1w_done"), sem("x1_half"), sem("x1_sum")
        m_ident, x2_in = sem("m_ident"), sem("x2_in")
        x1T_hi, x1T_lo = sem("x1T_hi"), sem("x1T_lo")
        hs_hi, hs_ready, ths_done, hsT_ready = sem("hs_hi"), sem("hs_ready"), sem("ths_done"), sem("hsT_ready")
        z1_done, wz_ready, twz_done = sem("z1_done"), sem("wz_ready"), sem("twz_done")
        wzT_hi, wzT_lo = sem("wzT_hi"), sem("wzT_lo")
        main_done, y_ready = sem("main_done"), sem("y_ready")
        y_out = sem("y_out")

        block = ctx.enter_context(nc.Block())

        def rows(t, k):
            return t[:, k * P:(k + 1) * P]

        def turn_rc(a, router, thi, tlo, c0, split, waits, router_first):
            units = []
            for k0, n in GROUPS:
                moves = []
                for j in range(n):
                    ao, ro = (j * RC + E, j * RC) if router_first else (j * RC, j * RC + ER)
                    moves += [(ao, ER, split(a, k0 + j)), (ro, E, split(router, k0 + j))]
                dst = [t[:, k0:k0 + n, c0:c0 + RC] for t in (thi, tlo)]
                units.append((moves, dst, (n * RC, "p (k c) -> p k c", dict(k=n)), 1.0, waits))
            return units

        def strided(t, j):
            return t[:, j::K]

        def by_j(t):
            return t[:, :].rearrange("p (e j r) -> p j e r", e=E, j=K)

        def j_first(t):
            return t[:, :].rearrange("p (j e r) -> p j e r", e=E, j=K)

        def turn_b(src, thi, tlo, scale, waits):
            return [([(i * P, P, rows(src, j0 + i)) for i in range(4)],
                     [t[:, :].rearrange("p (o j) -> p o j", j=K)[:, :, j0:j0 + 4] for t in (thi, tlo)],
                     (512, "p (j o) -> p o j", dict(j=4)), scale, waits) for j0 in (0, 4)]

        units_r0 = turn_rc(a0f, routers[:, 1, :], R0Thi, R0Tlo, 0, strided, [(a0f_in, 16), (r0_in, 16)], True)
        units_a0 = turn_rc(a0c, routers[:, 0, :], C0hi, C0lo, 0, rows, [(a0c_in, 16), (wr0_in, 16)], False)
        units_bw = turn_b(bw_j, BwThi, BwTlo, 1.0, [(bw_j_ready, 1)])
        units_b1 = turn_b(wraw[2], B1Thi, B1Tlo, 2.0, [(wraw_in[2], 16 * 8)])
        units_wb = []
        for o in range(K):
            for k0 in (0, 4):
                units_wb.append(([(i * P, P, rows(wraw[o % 4], k0 + i)) for i in range(4)],
                                 [t[:, k0:k0 + 4, RC + o * P:RC + (o + 1) * P] for t in (WbThi, WbTlo)],
                                 (512, "p (k c) -> p k c", dict(k=4)), 1.0,
                                 [(wraw_in[o % 4], 16 * (3 + o // 4))]))
        units_r1 = turn_rc(a0c, routers[:, 0, :], WbThi, WbTlo, 0, rows, [(a1_in, 16), (r1_in, 16)], True)
        units_bs = [([(i * P, P, rows(bwraw, k0 + i)) for i in range(4)],
                     [t[:, k0 * P:(k0 + 4) * P] for t in (ws_hi[1], ws_lo[1])],
                     (512, None, {}), 1.0, [(bs_in, 16 * NB)]) for k0 in (0, 4)]
        units_first = units_r0 + units_a0
        WB0 = 3
        units_second = units_wb[:2 * WB0] + units_r1 + units_bs + units_wb[2 * WB0:] + units_bw
        NU1 = len(units_first)
        NU2 = NU1 + len(units_second)
        NEF = NU1 + 2 * WB0 + len(units_r1) + len(units_bs)

        def wb_turned(o):
            return (NU1 if o < WB0 else NEF - 2 * WB0) + 2 * o + 2

        def unit_bank(q):
            return big[q % 3] if q < NU2 else (p0, pt)[q - NU2]

        def psum_of(q, unit):
            width, how, dims = unit[2]
            v = unit_bank(q)[:, 0:width]
            return v.rearrange(how, **dims) if how else v

        def split_of(hi, lo, k):
            return rows(hi, k), rows(lo, k)

        CHUNKS = [(0, RC + 2 * P), (RC + 2 * P, 4 * P), (RC + 6 * P, 2 * P)]
        WB_AT = 512 - 2 * P
        M_BANKS = [0, 5]

        def m_psum(bank, c):
            at = WB_AT - RC if c == 0 else 0
            return banks[:, bank + c, at:at + CHUNKS[c][1]]

        c0_sums = [t[:, 0:4 * RC].rearrange("p (k c) -> p k c", k=4) for t in (a0f, b1_j)]
        XT_BANKS = [(big[1], big[2]), (big[0], big[1])]
        XT_FIRST = [(pm[0], pm[1]), (pm[2], pm[0])]
        XT_EARLY = (p0, pt)
        X1W_BANKS, X1W_FIRST = [big[0], big[1], big[2], big[0]], [big[0], big[1], p0, pt]

        def quarter(t, g):
            return t[:, g * 4 * P:(g + 1) * 4 * P]

        def tile_of(t, k, half):
            return t[:, (2 * k + half) * P:(2 * k + half + 1) * P]

        def half_tiles(t, half, h):
            return t[:, :].rearrange("p (k c) -> p k c", k=K)[:, 4 * h:4 * h + 4, half * P:(half + 1) * P]

        def wait_earlier(eng, s, n):
            if not isinstance(n, int) or n > 0:
                eng.wait_ge(s, n)

        @block.sync
        def _(sp):
            sp.dma_start(a0f[:, :], A0f.rearrange("e r d -> (e r) d")).then_inc(a0f_in, 16)
            sp.dma_start(routers[:, 1, :], route_w).then_inc(r0_in, 16)
            w0v = W0.rearrange("(p j) i -> p j i", j=K)

            def load_b(raw, src, s):
                sp.dma_start(raw[:, :].rearrange("p (e c) -> p e c", e=E),
                             src.rearrange("e (p j) r -> p e (j r)", j=K)).then_inc(s, 16)

            for j in range(K):
                if j >= 4:
                    sp.wait_ge(w0_hi, j - 3)
                    sp.wait_ge(w0_lo, j - 3)
                sp.dma_start(wraw[j % 4][:, :], w0v[:, j, :]).then_inc(wraw_in[j % 4], 16)
                if j == 3:
                    sp.dma_start(routers[:, 0, :], Wr0).then_inc(wr0_in, 16)
                if j == 5:
                    load_b(b0raw, B0, b0_in)
            sp.dma_start(xin_first[:, :].rearrange("p (t d) -> p t d", t=2),
                         xf[0:2 * P, :].rearrange("(t p) d -> p t d", p=P)).then_inc(x0_in, 16)
            sp.dma_start(a0c[:, :], A0c.rearrange("e r d -> (e r) d")).then_inc(a0c_in, 16)
            load_b(bwraw, Bw, bw_in)
            sp.dma_start(brow[:, :], b1.rearrange("(k p) -> k p", k=K)).then_inc(brow_in, 16)
            for o in range(K):
                if o < 4:
                    sp.wait_ge(w0_hi, o + 5)
                    sp.wait_ge(w0_lo, o + 5)
                else:
                    sp.wait_ge(unit_done, wb_turned(o - 4))
                sp.dma_start(wraw[o % 4][:, :], Wb[o * P:(o + 1) * P, :]).then_inc(wraw_in[o % 4], 16)
                if o == 3:
                    sp.wait_ge(b0_lo, 1)
                    load_b(b0raw, B1, b1_in)
                    sp.wait_ge(ids_in, 32)
                    sp.wait_ge(bw_j_ready, 1)
                    for b in range(NB):
                        slot = sp.value_load(ids[0:1, NB + b:NB + b + 1], min_val=0, max_val=lora_Bs.shape[0] - 1)
                        sp.dma_start(bwraw[b * R:(b + 1) * R, :],
                                     lora_Bs[bass.ds(slot, 1), :, :].rearrange("s r d -> (s r) d")).then_inc(bs_in, 16)
            w1v = W1.rearrange("(m p) i -> p m i", p=P)

            def load_w1(tile, buffer):
                sp.dma_start(wraw[buffer][:, :].rearrange("p (m c) -> p m c", m=K),
                             w1v[:, :, bass.ds(tile * P, P)]).then_inc(wraw_in[buffer], 16)

            for n in range(4):
                sp.wait_ge(unit_done, wb_turned(4 + n))
                load_w1(n, n)
            sp.wait_ge(b1_j_ready, 1)
            sp.dma_start(b1_dram, b1_j[:, :]).then_inc(b1_stored, 16)
            sp.wait_ge(fe_hi, 3)
            sp.wait_ge(fe_lo, 3)
            sp.dma_start(fe_hi_dram[0:P, :], Mhi[:, K - 1, R:MW].bitcast(F32)).then_inc(fe_stored, 16)
            sp.dma_start(fe_lo_dram[0:P, :], Mlo[:, K - 1, R:MW].bitcast(F32)).then_inc(fe_stored, 16)
            sp.wait_ge(fe_stored, 32)
            sp.dma_start(x2_early[:, :], xf[2 * P:3 * P, :]).then_inc(x2_in, 16)
            sp.wait_ge(acc_step, 1)
            sp.dma_start(b_acc[0:1, RC:MC], b_base.rearrange("(a o) -> a o", a=1)).then_inc(bbase_in, 16)
            sp.wait_ge(x1_sum, 4)
            sp.dma_start(x1T_dram, xin_first[:, :]).then_inc(x1_stored, 16)
            with sp.Fori(2, K // 2) as i:
                for par in range(2):
                    sp.wait_ge(w1_hi, i * 2 + par - 1)
                    sp.wait_ge(w1_lo, i * 2 + par - 1)
                    load_w1(i * 2 + par, 2 + par)

            blocks = [(0, fe_hi_dram), (32, fe_lo_dram), (64, fe_hi_dram)]

            def load_e(b):
                for p, src in blocks:
                    sp.dma_start(Ebuf[p:p + R, :].bitcast(F32), src[bass.ds(b * R, R), 0:RC]).then_inc(e_in, 16)

            def load_f(b):
                for p, src in blocks:
                    sp.dma_start(Fbuf[p:p + R, :].bitcast(F32), src[bass.ds(b * R, R), RC:MC]).then_inc(f_in, 16)

            def load_as(b, guard):
                slot = sp.value_load(ids[0:1, bass.ds(NB + b, 1)], min_val=0, max_val=lora_As.shape[0] - 1)
                src = lora_As[bass.ds(slot, 1), :, :].rearrange("s (k p) r -> p (s k) r", p=P)
                if guard:
                    sp.wait_ge(as_hi, b)
                    sp.wait_ge(as_lo, b)
                sp.dma_start(asraw[:, :, :], src).then_inc(as_in, 16)

            def load_x(t, turn):
                sp.dma_start(xin[turn][:, :], xf[bass.ds(t * P, P), :]).then_inc(x_in[turn], 16)

            sp.wait_ge(w1_hi, K - 1)
            sp.wait_ge(w1_lo, K - 1)
            sp.wait_ge(b1_stored, 16)
            sp.dma_start(wraw[2][:, :], b1_dram).then_inc(wraw_in[2], 16)
            sp.wait_ge(w1_hi, K)
            sp.wait_ge(w1_lo, K)
            sp.wait_ge(x1_stored, 16)
            sp.dma_start(wraw[3][:, :], x1T_dram[:, D:2 * D]).then_inc(wraw_in[3], 16)
            load_as(0, False)
            sp.wait_ge(unit_done, NU2 + 2)
            sp.dma_start(wraw[2][:, :], x1T_dram[:, 0:D]).then_inc(wraw_in[2], 16)
            sp.wait_ge(brow_hi, 3)
            sp.wait_ge(brow_lo, 3)
            sp.dma_start(fe_hi_dram[P:P + 1, :], Mhi[0:1, K - 1, R:MW].bitcast(F32)).then_inc(fe_stored, 16)
            sp.dma_start(fe_lo_dram[P:P + 1, :], Mlo[0:1, K - 1, R:MW].bitcast(F32)).then_inc(fe_stored, 16)
            sp.wait_ge(m_done, 3 * K)
            load_x(3, 1)
            load_x(4, 0)
            sp.wait_ge(fe_stored, 64)
            sp.wait_ge(memsets_done, 3)
            load_e(0)
            load_f(0)
            for p, src in blocks[0:2]:
                sp.dma_start(Ebuf[p + R:p + R + 1, :].bitcast(F32), src[P:P + 1, 0:RC]).then_inc(e_in, 16)
                sp.dma_start(Fbuf[p + R:p + R + 1, :].bitcast(F32), src[P:P + 1, RC:MC]).then_inc(f_in, 16)

            def slot_dmas(b, last, more_x):
                def store(half):
                    sp.wait_ge(y_ready, b * 6 + half * 3 + 3)
                    sp.dma_start(outf[bass.ds(b * 2 * P + half * P, P), :], ybuf[:, :]).then_inc(y_out, 16)

                if not last:
                    load_as(b + 1, True)
                store(0)
                if last:
                    for c, (y0, n) in enumerate(Y_OF):
                        sp.wait_ge(y_ready, (NT - 1) * 3 + c + 1)
                        sp.dma_start(outf[(NT - 1) * P:NT * P, y0:y0 + n], ybuf[:, y0:y0 + n]).then_inc(y_out, 16)
                    return
                sp.wait_ge(z1_done, b * 2 + 2)
                load_e(b + 1)
                store(1)
                load_f(b + 1)
                if more_x:
                    for half in range(2):
                        sp.wait_ge(tx_done, b * 4 + 10 + half * 2)
                        load_x(b * 2 + 6 + half, half)

            sp.wait_ge(tx_done, 8)
            load_x(5, 1)
            slot_dmas(0, False, True)
            with sp.Fori(1, NB - 3) as i:
                slot_dmas(i, False, True)
            for b in range(NB - 3, NB):
                slot_dmas(b, b == NB - 1, False)
            sp.wait_ge(y_out, 16 * (NT - 1 + len(Y_OF)))

        @block.gpsimd
        def _(gp):
            gp.memset(ident[:, :], 0.0).then_inc(gp_step, 1)
            gp.wait_ge(gp_step, 1)
            gp.affine_select(out=ident[:, :], in_=ident[:, :], compare_op=ALU.not_equal, fill=1.0,
                             base=0, pattern=[[-1, P]], channel_multiplier=1).then_inc(ident_ready, 1)
            gp.dma_start(ids[0:1, 0:NB], lang_ids.rearrange("(a b) -> a b", a=1)).then_inc(ids_in, 16)
            gp.dma_start(ids[0:1, NB:2 * NB], slot_ids.rearrange("(a b) -> a b", a=1)).then_inc(ids_in, 16)
            gp.dma_start(lang[:, :], lang_ids.rearrange("(a b) -> a b", a=1).broadcast_to([P, NB])).then_inc(lang_in, 16)
            gp.iota(iota[:, :], pattern=[[1, E]], base=0, channel_multiplier=0,
                    allow_small_or_imprecise_dtypes=True).then_inc(gp_step, 1)
            gp.memset(ones[:, :], 1.0).then_inc(gp_step, 1)
            gp.wait_ge(bw_in, 16)
            gp.tensor_copy(j_first(bw_j), by_j(bwraw)).then_inc(bw_j_ready, 1)
            for g in range(2):
                gp.wait_ge(c0_hi, g + 1)
                c0 = slice(4 * g, 4 * g + 4)
                gp.tensor_tensor(C0lo[:, c0, ER + E:C0C], c0_sums[g], C0hi[:, c0, ER + E:C0C].bitcast(F32),
                                 ALU.subtract).then_inc(c0_lo, 1)
            gp.wait_ge(unit_done, 6)
            gp.dma_start(a0c[:, :], A1.rearrange("e r d -> (e r) d")).then_inc(a1_in, 16)
            gp.dma_start(routers[:, 0, :], W_router).then_inc(r1_in, 16)
            gp.wait_ge(c0_lo, 2)
            gp.wait_ge(b1_in, 16)
            gp.tensor_copy(j_first(b1_j), by_j(b0raw)).then_inc(b1_j_ready, 1)
            gp.wait_ge(m_done, 3 * K)
            gp.memset(Fbuf[:, :].bitcast(F32), 0.0).then_inc(memsets_done, 1)

        @block.scalar
        def _(act):
            def copy_units(q0, units):
                for q, unit in enumerate(units, q0):
                    act.wait_ge(unit_done, q + 1)
                    act.activation(unit[1][0], psum_of(q, unit), ACT.Copy, scale=unit[3]).then_inc(unit_hi, 1)

            def hi_half(done, nth, dst, src, ready):
                act.wait_ge(done, nth)
                act.activation(dst, src, ACT.Copy).then_inc(ready, 1)

            copy_units(0, units_r0[0:1])
            for j in range(K):
                act.wait_ge(wraw_in[j % 4], 16 * (j // 4 + 1))
                if j >= 4:
                    act.wait_ge(w0_used, j - 3)
                act.activation(w0s_hi[j % 4][:, :], wraw[j % 4][:, :], ACT.Copy).then_inc(w0_hi, 1)
                if j == 0:
                    copy_units(1, units_r0[1:3])
                if j == 6:
                    act.wait_ge(b0_in, 16)
                    act.activation(j_first(b0hi), by_j(b0raw), ACT.Copy).then_inc(b0_hi, 1)
            for g in range(2):
                if g == 0:
                    act.wait_ge(c0_done, 1)
                else:
                    act.wait_ge(w0_used, K)
                act.activation(c0_sums[g], banks[:, 4 * g:4 * g + 4, RC:2 * RC], ACT.Copy).then_inc(c0_half, 1)
            for g in range(2):
                act.wait_ge(c0_sum, g + 1)
                act.activation(C0hi[:, 4 * g:4 * g + 4, ER + E:C0C], c0_sums[g], ACT.Copy).then_inc(c0_hi, 1)
            def xT_part(t, half, xT, at, guard):
                if guard:
                    act.wait_ge(p0_done, t - 1)
                    act.wait_ge(x1_sum, (t - half) * 2)
                for h in range(2):
                    hi_half(tx_done, t * 2 + h + 1, half_tiles(xT[0], half, h),
                            at[h].rearrange("p (k c) -> p k c", k=4), xT_hi)

            xT_part(0, 0, xT_first, XT_FIRST[0], False)
            act.wait_ge(d0w_done, 1)
            act.activation(D0hi[:, :], p0[:, 0:RC], ACT.Copy, scale=2.0).then_inc(d0w_hi, 1)
            copy_units(3, units_a0)

            def exp0(t):
                act.wait_ge(max0_ready, t + 1)
                act.activation(G0["ex"][:, :], G0["mx"][:, 0:1], ACT.Exp, bias=G0["mx"][:, 1:2], scale=-1.0)\
                   .then_inc(exp0_ready, 1)

            def exp1(t):
                act.wait_ge(max1_ready, t + 1)
                act.activation(G1["ex"][:, :], G1["mx"][:, 0:1], ACT.Exp, bias=G1["mx"][:, 1:2], scale=-1.0)\
                   .then_inc(exp1_ready, 1)

            def hgT_part(t):
                wait_earlier(act, z0_done, t)
                hi_half(thg_done, t + 1, hgThi[:, :], pt_hg, hgT_hi)

            def whT_part(t, half):
                wait_earlier(act, x1w_done, (t - half) * 2)
                hi_half(twh_done, t + 1, whThi[:, half * P:(half + 1) * P], pt_wh, whT_hi)

            def x1T_part(q, turn, g, src):
                if g == 0:
                    wait_earlier(act, main_done, q * 6 - 6)
                hi_half(x1_sum, q * 4 + g + 1, quarter(x1T[turn][0], g), src, x1T_hi)

            def y_part(t, c):
                y0, n = Y_OF[c]
                act.wait_ge(main_done, t * 3 + c + 1)
                if c == 0:
                    wait_earlier(act, y_out, t * 16)
                act.activation(ybuf[:, y0:y0 + n], pm[c][:, PART - n:PART], ACT.Copy).then_inc(y_ready, 1)

            def hsT_part(t):
                wait_earlier(act, main_done, t * 3)
                hi_half(ths_done, t + 1, hsT[:, :], pt_h1[0:96, :], hsT_ready)

            def wzT_part(t):
                wait_earlier(act, main_done, t * 3)
                hi_half(twz_done, t + 1, wzThi[:, :], pt_wz, wzT_hi)

            def as_part(b):
                act.wait_ge(as_in, b * 16 + 16)
                wait_earlier(act, h1_done, b * 2)
                act.activation(Mhi[:, :, 0:R], asraw[:, :, :], ACT.Copy).then_inc(as_hi, 1)

            def keep_fe(c):
                c0, n = CHUNKS[c]
                act.wait_ge(fe_done, c + 1)
                act.activation(Mhi[:, K - 1, R + c0:R + c0 + n], m_psum(0, c), ACT.Copy, scale=2.0).then_inc(fe_hi, 1)

            copy_units(NU1, units_second[:NEF - NU1])
            exp0(0)
            copy_units(NEF, units_second[NEF - NU1:NEF - NU1 + 4])
            hgT_part(0)
            copy_units(NEF + 4, units_second[NEF - NU1 + 4:NEF - NU1 + 8])
            keep_fe(0)
            copy_units(NEF + 8, units_second[NEF - NU1 + 8:NEF - NU1 + 10])
            xT_part(1, 1, xT_first, XT_FIRST[1], False)
            whT_part(0, 0)
            copy_units(NEF + 10, units_bw)
            exp0(1)
            act.wait_ge(wraw_in[0], 80)
            act.activation(ws_hi[0][:, :], wraw[0][:, :], ACT.Copy).then_inc(w1_hi, 1)
            keep_fe(1)
            hgT_part(1)
            keep_fe(2)
            act.wait_ge(wraw_in[1], 80)
            act.activation(ws_hi[1][:, :], wraw[1][:, :], ACT.Copy).then_inc(w1_hi, 1)
            whT_part(1, 1)
            act.wait_ge(w1_lo, 2)
            act.wait_ge(b1_stored, 16)
            act.wait_ge(x1_stored, 16)
            act.wait_ge(fe_stored, 32)

            def keep_m(i, par, chunks=range(3)):
                for c in chunks:
                    c0, n = CHUNKS[c]
                    if len(chunks) == 2:
                        act.wait_ge(m_done, i * 6 + par * 3 + c + 1)
                    else:
                        act.wait_ge(m_ident, i * 2 + par + 1)
                    act.activation(Mhi[:, bass.ds(i * 2 + par, 1), R + c0:R + c0 + n],
                                   m_psum(M_BANKS[par], c).unsqueeze(1), ACT.Copy).then_inc(m_hi, 1)

            with act.Fori(0, K // 2 - 1) as i:
                for par in range(2):
                    keep_m(i, par)
                    act.wait_ge(wraw_in[2 + par], i * 16 + 16 * 5)
                    act.activation(ws_hi[par][:, :], wraw[2 + par][:, :], ACT.Copy).then_inc(w1_hi, 1)
            keep_m(K // 2 - 1, 0)
            copy_units(NU2, units_b1)
            as_part(0)
            for c, (c0, n) in enumerate(CHUNKS):
                act.wait_ge(bias_done, c + 1)
                act.activation(Mhi[0:1, K - 1, R + c0:R + c0 + n], m_psum(0, c)[0:1, :], ACT.Copy)\
                   .then_inc(brow_hi, 1)
            act.wait_ge(fe_stored, 64)
            keep_m(K // 2 - 1, 1, (0, 1))
            act.wait_ge(m_done, 3 * K)
            for g in range(4):
                if g == 2:
                    xT_part(2, 0, xT_main, XT_EARLY, False)
                if g == 0:
                    act.wait_ge(wraw_in[2], 16 * 9)
                    act.wait_ge(wraw_in[3], 16 * 8)
                x1T_part(0, 0, g, quarter(wraw[2 + g // 2], g % 2))
            keep_m(K // 2 - 1, 1, (2,))

            def slot(b, turn, has_a, has_n, first=False):
                m, a, n, q = b * 2, b * 2 + 2, b * 2 + 4, b + 1
                if has_a:
                    exp0(a)
                    hgT_part(a)
                hsT_part(m)
                if first:
                    xT_part(a + 1, 1, xT_main, XT_BANKS[1], False)
                exp1(m)
                if has_a:
                    whT_part(a, 0)
                    exp0(a + 1)
                wzT_part(m)
                y_part(m, 0)
                y_part(m, 1)
                if has_a:
                    hgT_part(a + 1)
                y_part(m, 2)
                if has_a:
                    whT_part(a + 1, 1)
                    x1T_part(q, 1 - turn, 0, quarter(x1_sums, 0))
                hsT_part(m + 1)
                if has_a:
                    x1T_part(q, 1 - turn, 1, quarter(x1_sums, 1))
                    x1T_part(q, 1 - turn, 2, quarter(x1_sums, 2))
                exp1(m + 1)
                if has_a:
                    x1T_part(q, 1 - turn, 3, quarter(x1_sums, 3))
                if has_n:
                    xT_part(n, 0, xT_main, XT_BANKS[0], True)
                wzT_part(m + 1)
                y_part(m + 1, 0)
                y_part(m + 1, 1)
                if has_n:
                    xT_part(n + 1, 1, xT_main, XT_BANKS[1], True)
                if has_a:
                    as_part(b + 1)
                y_part(m + 1, 2)
            slot(0, 0, True, True, first=True)
            with act.Fori(0, 2) as i:
                for turn in (1, 0):
                    slot(i * 2 + 2 - turn, turn, True, True)
            slot(NB - 3, 1, True, True)
            slot(NB - 2, 0, True, False)
            slot(NB - 1, 1, False, False)

        @block.vector
        def _(dve):
            def lo(out_, src, hi, scale=1.0):
                return dve.scalar_tensor_tensor(out=out_, in0=src, scalar=scale, in1=hi.bitcast(F32),
                                                op0=ALU.mult, op1=ALU.subtract)

            def lo_units(q0, units):
                for q, unit in enumerate(units, q0):
                    dve.wait_ge(unit_hi, q + 1)
                    lo(unit[1][1], psum_of(q, unit), unit[1][0], unit[3]).then_inc(unit_lo, 1)

            dve.memset(hs[:, :].bitcast(F32), 0.0).then_inc(bias_step, 1)
            dve.memset(Ebuf[:, :].bitcast(F32), 0.0).then_inc(memsets_done, 1)
            dve.wait_ge(bias_step, 1)
            dve.memset(hs[:, R:R + 1].bitcast(F32), 1.0).then_inc(memsets_done, 1)
            dve.memset(hs[:, 32 + R:32 + R + 1].bitcast(F32), 1.0).then_inc(bias_step, 1)
            lo_units(0, units_r0[0:1])
            for j in range(K):
                dve.wait_ge(w0_hi, j + 1)
                if j >= 4:
                    dve.wait_ge(w0_used, j - 3)
                lo(w0s_lo[j % 4][:, :], wraw[j % 4][:, :], w0s_hi[j % 4][:, :]).then_inc(w0_lo, 1)
                if j == 0:
                    lo_units(1, units_r0[1:3])
                if j == 6:
                    dve.wait_ge(b0_hi, 1)
                    for i in range(K):
                        ins = lo(j_first(b0lo)[:, i], by_j(b0raw)[:, i], j_first(b0hi)[:, i])
                    ins.then_inc(b0_lo, 1)
            dve.wait_ge(lang_in, 16)
            dve.tensor_copy(langf[:, :], lang[:, :]).then_inc(bias_step, 1)
            dve.wait_ge(bias_step, 3)
            dve.wait_ge(gp_step, 2)
            for b in range(NB):
                dve.tensor_scalar(bias[:, b * E:(b + 1) * E], iota[:, :], langf[:, b:b + 1], LANG_BIAS,
                                  ALU.is_equal, ALU.mult).then_inc(bias_step, 1)
            for g in range(2):
                dve.wait_ge(c0_half, g + 1)
                dve.tensor_tensor(c0_sums[g], banks[:, 4 * g:4 * g + 4, 0:RC], c0_sums[g], ALU.add).then_inc(c0_sum, 1)
            def xT_part(t, half, xT, at):
                for h in range(2):
                    dve.wait_ge(xT_hi, t * 2 + h + 1)
                    lo(half_tiles(xT[1], half, h), at[h].rearrange("p (k c) -> p k c", k=4),
                       half_tiles(xT[0], half, h)).then_inc(xT_lo, 1)

            xT_part(0, 0, xT_first, XT_FIRST[0])
            dve.wait_ge(d0w_hi, 1)
            lo(D0lo[:, :], p0[:, 0:RC], D0hi[:, :], 2.0).then_inc(d0w_lo, 1)
            lo_units(3, units_a0)

            G_STEPS = 8

            def iota_there():
                dve.wait_ge(gp_step, 2)

            def spread(out_, h, g):
                return dve.tensor_tensor(out_.rearrange("p (e r) -> p e r", e=E), h.rearrange("p (e r) -> p e r", e=E),
                                         g[:, :].unsqueeze(2).broadcast_to([P, E, R]), ALU.mult)

            def gates0(t, b, meanwhile=None):
                dve.wait_ge(p0_done, t + 1)
                dve.tensor_tensor(G0["lg"][:, :], p0[:, ER:ER + E], bias[:, bass.ds(b * E, E)], ALU.add).then_inc(lg0_ready, 1)
                iota_there()
                dve.wait_ge(lg0_ready, t + 1)
                gates_from(G0, G0["lg"][:, :], t, g0_step, max0_ready, exp0_ready, meanwhile)
                wait_earlier(dve, thg_done, t)
                spread(hg[:, :], p0[:, 0:ER], G0["g"]).then_inc(hg_ready, 1)

            def gates_from(G, logits, t, step, max_ready, exp_ready, meanwhile=None):
                def at(n):
                    dve.wait_ge(step, t * G_STEPS + n)
                dve.max(G["mx"][:, :], logits).then_inc(max_ready, 1)
                iota_there()
                dve.wait_ge(max_ready, t + 1)
                dve.max_index(G["ix"][:, :], G["mx"][:, :], logits).then_inc(step, 1)
                at(1)
                dve.tensor_copy(G["ixf"][:, :], G["ix"][:, 0:2]).then_inc(step, 1)
                if meanwhile:
                    meanwhile()
                dve.wait_ge(exp_ready, t + 1)
                dve.tensor_scalar(G["den"][:, :], G["ex"][:, :], 1.0, None, ALU.add).then_inc(step, 1)
                at(3)
                dve.reciprocal(G["w"][:, 0:1], G["den"][:, :]).then_inc(step, 1)
                at(4)
                dve.tensor_tensor(G["w"][:, 1:2], G["ex"][:, :], G["w"][:, 0:1], ALU.mult).then_inc(step, 1)
                dve.tensor_scalar(G["ga"][:, :], iota[:, :], G["ixf"][:, 0:1], G["w"][:, 0:1],
                                  ALU.is_equal, ALU.mult).then_inc(step, 1)
                at(5)
                dve.tensor_scalar(G["gb"][:, :], iota[:, :], G["ixf"][:, 1:2], G["w"][:, 1:2],
                                  ALU.is_equal, ALU.mult).then_inc(step, 1)
                at(7)
                dve.tensor_tensor(G["g"][:, :], G["ga"][:, :], G["gb"][:, :], ALU.add).then_inc(step, 1)
                at(8)

            def gates1(t, meanwhile):
                dve.wait_ge(z1_done, t + 1)
                dve.tensor_copy(G1["lg"][:, :], pm[0][:, R:R + E]).then_inc(lg1_ready, 1)
                iota_there()
                dve.wait_ge(lg1_ready, t + 1)
                gates_from(G1, G1["lg"][:, :], t, g1_step, max1_ready, exp1_ready, meanwhile)
                wait_earlier(dve, twz_done, t)
                spread(wz[:, :], pm[0][:, R + E:ZC], G1["g"]).then_inc(wz_ready, 1)

            def top1(t):
                TOP = 3

                def at(n):
                    dve.wait_ge(top_step, t * TOP + n)
                z = ER + E
                dve.wait_ge(z0_done, t + 1)
                dve.tensor_copy(GT["lg"][:, :], p0[:, z:z + E]).then_inc(lgt_ready, 1)
                iota_there()
                dve.wait_ge(lgt_ready, t + 1)
                dve.max(GT["mx"][:, :], GT["lg"][:, :]).then_inc(maxt_ready, 1)
                iota_there()
                dve.wait_ge(maxt_ready, t + 1)
                dve.max_index(GT["ix"][:, :], GT["mx"][:, :], GT["lg"][:, :]).then_inc(top_step, 1)
                at(1)
                dve.tensor_copy(GT["ixf"][:, :], GT["ix"][:, 0:2]).then_inc(top_step, 1)
                at(2)
                dve.tensor_scalar(GT["g"][:, :], iota[:, :], GT["ixf"][:, 0:1], GT["mx"][:, 0:1],
                                  ALU.is_equal, ALU.mult).then_inc(top_step, 1)
                at(3)
                wait_earlier(dve, twh_done, t)
                spread(wh[:, :], p0[:, z + E:C0C], GT["g"]).then_inc(wh_ready, 1)

            def hgT_part(t):
                dve.wait_ge(hgT_hi, t + 1)
                lo(hgTlo[:, :], pt_hg, hgThi[:, :]).then_inc(hgT_lo, 1)

            def whT_part(t, half):
                dve.wait_ge(whT_hi, t + 1)
                s = slice(half * P, (half + 1) * P)
                lo(whTlo[:, s], pt_wh, whThi[:, s]).then_inc(whT_lo, 1)

            def wzT_part(t):
                dve.wait_ge(wzT_hi, t + 1)
                lo(wzTlo[:, :], pt_wz, wzThi[:, :]).then_inc(wzT_lo, 1)

            def x1_add(q, g, bank, xT, sums):
                dve.wait_ge(x1w_done, q * 4 + g + 1)
                wait_earlier(dve, x1T_hi, q * 4 + g - 3)
                dve.tensor_tensor(quarter(sums, g), bank, quarter(xT[1], g).bitcast(F32), ALU.add).then_inc(x1_half, 1)
                dve.wait_ge(x1_half, q * 4 + g + 1)
                dve.tensor_tensor(quarter(sums, g), quarter(sums, g), quarter(xT[0], g).bitcast(F32), ALU.add)\
                   .then_inc(x1_sum, 1)

            def x1T_part(q, turn, g, src):
                dve.wait_ge(x1T_hi, q * 4 + g + 1)
                lo(quarter(x1T[turn][1], g), src, quarter(x1T[turn][0], g)).then_inc(x1T_lo, 1)

            def hs_part(t):
                dve.wait_ge(h1_done, t + 1)
                wait_earlier(dve, ths_done, t)
                dve.tensor_copy(hs[:, 0:64].rearrange("p (b c) -> p b c", b=2)[:, :, 0:R],
                                pm[0][:, 0:R].unsqueeze(1).broadcast_to([P, 2, R])).then_inc(hs_hi, 1)
                dve.wait_ge(hs_hi, t + 1)
                lo(hs[:, 64:64 + R], pm[0][:, 0:R], hs[:, 0:R]).then_inc(hs_ready, 1)

            def as_part(b):
                dve.wait_ge(as_hi, b + 1)
                lo(Mlo[:, :, 0:R], asraw[:, :, :], Mhi[:, :, 0:R]).then_inc(as_lo, 1)

            def keep_fe(c):
                c0, n = CHUNKS[c]
                dve.wait_ge(fe_hi, c + 1)
                lo(Mlo[:, K - 1, R + c0:R + c0 + n], m_psum(0, c), Mhi[:, K - 1, R + c0:R + c0 + n], 2.0)\
                    .then_inc(fe_lo, 1)

            dve.wait_ge(bias_step, 3 + NB)
            lo_units(NU1, units_second[:NEF - NU1])
            dve.wait_ge(bcol_turned, 1)
            dve.tensor_copy(bcol[:, :], pt[:, 0:K]).then_inc(bcol_ready, 1)
            gates0(0, 0)
            lo_units(NEF, units_second[NEF - NU1:NEF - NU1 + 4])
            hgT_part(0)
            lo_units(NEF + 4, units_second[NEF - NU1 + 4:NEF - NU1 + 8])
            keep_fe(0)
            top1(0)
            lo_units(NEF + 8, units_second[NEF - NU1 + 8:NEF - NU1 + 10])
            xT_part(1, 1, xT_first, XT_FIRST[1])
            whT_part(0, 0)
            lo_units(NEF + 10, units_bw)
            gates0(1, 0)
            dve.wait_ge(w1_hi, 1)
            lo(ws_lo[0][:, :], wraw[0][:, :], ws_hi[0][:, :]).then_inc(w1_lo, 1)
            keep_fe(1)
            hgT_part(1)
            top1(1)
            keep_fe(2)
            dve.wait_ge(w1_hi, 2)
            lo(ws_lo[1][:, :], wraw[1][:, :], ws_hi[1][:, :]).then_inc(w1_lo, 1)
            dve.wait_ge(fe_stored, 32)
            dve.memset(b_acc[:, :], 0.0).then_inc(acc_step, 1)
            whT_part(1, 1)
            for g in range(4):
                x1_add(0, g, X1W_FIRST[g], xT_first, xin_first)
            dve.wait_ge(bcol_ready, 1)
            dve.wait_ge(bbase_in, 16)

            def b_times(k, nth):
                for n, t in enumerate((WbThi, WbTlo)):
                    dve.wait_ge(acc_step, nth * 2 + n + 1)
                    dve.scalar_tensor_tensor(out=b_acc[:, :].unsqueeze(1), in0=t[:, bass.ds(k, 1), :].bitcast(F32),
                                             scalar=bcol[:, bass.ds(k, 1)], in1=b_acc[:, :].unsqueeze(1),
                                             op0=ALU.mult, op1=ALU.add).then_inc(acc_step, 1)

            def keep_m(i, par, chunks=range(3)):
                for c in chunks:
                    c0, n = CHUNKS[c]
                    dve.wait_ge(m_hi, i * 6 + par * 3 + c + 1)
                    lo(Mlo[:, bass.ds(i * 2 + par, 1), R + c0:R + c0 + n], m_psum(M_BANKS[par], c).unsqueeze(1),
                       Mhi[:, bass.ds(i * 2 + par, 1), R + c0:R + c0 + n]).then_inc(m_lo, 1)

            flat = banks[:, :, :].rearrange("p b c -> p (b c)")

            def add_ident(i, par):
                dve.wait_ge(m_done, i * 6 + par * 3 + 3)
                block = flat[:, bass.ds(M_BANKS[par] * 512 + WB_AT + par * P + i * (2 * P), P)]
                dve.tensor_tensor(block, block, ident[:, :], ALU.add).then_inc(m_ident, 1)

            with dve.Fori(0, K // 2 - 1) as i:
                for par in range(2):
                    add_ident(i, par)
                    keep_m(i, par)
                    dve.wait_ge(w1_hi, i * 2 + 3 + par)
                    lo(ws_lo[par][:, :], wraw[2 + par][:, :], ws_hi[par][:, :]).then_inc(w1_lo, 1)
                    b_times(i * 2 + par, i * 2 + par)
            b_times(K - 2, K - 2)
            b_times(K - 1, K - 1)
            add_ident(K // 2 - 1, 0)
            keep_m(K // 2 - 1, 0)
            lo_units(NU2, units_b1)
            as_part(0)
            for c, (c0, n) in enumerate(CHUNKS):
                dve.wait_ge(brow_hi, c + 1)
                lo(Mlo[0:1, K - 1, R + c0:R + c0 + n], m_psum(0, c)[0:1, :], Mhi[0:1, K - 1, R + c0:R + c0 + n])\
                    .then_inc(brow_lo, 1)
            dve.wait_ge(fe_stored, 64)
            keep_m(K // 2 - 1, 1, (0, 1))
            for g in range(4):
                if g == 2:
                    xT_part(2, 0, xT_main, XT_EARLY)
                x1T_part(0, 0, g, quarter(wraw[2 + g // 2], g % 2))
            add_ident(K // 2 - 1, 1)
            keep_m(K // 2 - 1, 1, (2,))

            def slot(b, turn, has_a, has_n, first=False):
                m, a, n, q = b * 2, b * 2 + 2, b * 2 + 4, b + 1

                def add(g):
                    x1_add(q, g, X1W_BANKS[g], xT_main, x1_sums)

                def split(g):
                    x1T_part(q, 1 - turn, g, quarter(x1_sums, g))

                if has_a:
                    gates0(a, q)
                    hgT_part(a)
                hs_part(m)
                if has_a:
                    top1(a)
                    if first:
                        xT_part(a + 1, 1, xT_main, XT_BANKS[1])
                    gates1(m, lambda: whT_part(a, 0))
                    gates0(a + 1, q, lambda: wzT_part(m))
                    hgT_part(a + 1)
                    top1(a + 1)
                    whT_part(a + 1, 1)
                    add(0)
                    hs_part(m + 1)
                    add(1)
                    split(0)
                    add(2)
                    gates1(m + 1, lambda: add(3))
                    split(1)
                    wzT_part(m + 1)
                    split(2)
                    split(3)
                else:
                    gates1(m, None)
                    wzT_part(m)
                    hs_part(m + 1)
                    gates1(m + 1, None)
                    wzT_part(m + 1)
                if has_n:
                    xT_part(n, 0, xT_main, XT_BANKS[0])
                    xT_part(n + 1, 1, xT_main, XT_BANKS[1])
                if has_a:
                    as_part(q)
            slot(0, 0, True, True, first=True)
            with dve.Fori(0, 2) as i:
                for turn in (1, 0):
                    slot(i * 2 + 2 - turn, turn, True, True)
            slot(NB - 3, 1, True, True)
            slot(NB - 2, 0, True, False)
            slot(NB - 1, 1, False, False)

        @block.tensor
        def _(pe):
            def turn_units(q0, units):
                for q, unit in enumerate(units, q0):
                    for s, v in unit[4]:
                        pe.wait_ge(s, v)
                    if q >= 3:
                        pe.wait_ge(unit_lo, q - 2)
                    for col, width, src in unit[0]:
                        kp = src.shape[0]
                        ins = pe.transpose(unit_bank(q)[:, col:col + width], src, ident[0:kp, 0:kp])
                    ins.then_inc(unit_done, 1)

            def three(out_, l, r, start, stop, **kw):
                pe.matmul(out_, l[0], r[0], start=start, stop=False, **kw)
                pe.matmul(out_, l[0], r[1], start=False, stop=False, **kw)
                return pe.matmul(out_, l[1], r[0], start=False, stop=stop, **kw)

            pe.wait_ge(ident_ready, 1)
            turn_units(0, units_r0)
            for j in range(K):
                pe.wait_ge(unit_lo, j // 3 + 1)
                pe.wait_ge(w0_lo, j + 1)
                for k in range(K):
                    if j == 0 and k == K - 3:
                        pe.wait_ge(unit_lo, 3)
                    for n, w in enumerate(split_of(w0s_hi[j % 4], w0s_lo[j % 4], k)):
                        ins = pe.matmul(banks[:, k, 0:2 * RC], w, R0T[:, j, :], start=j == 0 and n == 0,
                                        stop=j == K - 1 and n == 1)
                    if j == K - 1 and k == K // 2 - 1:
                        ins.then_inc(c0_done, 1)
                ins.then_inc(w0_used, 1)

            def turn_x(src, at):
                for h in range(2):
                    for k in range(4):
                        ins = pe.transpose(rows(at[h], k), rows(src, 4 * h + k), ident[:, :])
                    ins.then_inc(tx_done, 1)

            pe.wait_ge(c0_sum, 1)
            pe.wait_ge(x0_in, 16)
            turn_x(xin_first[:, 0:D], XT_FIRST[0])
            pe.wait_ge(b0_lo, 1)
            for j in range(K):
                ins = three(p0[:, 0:RC], split_of(b0hi, b0lo, j), (R0Thi[:, j, :], R0Tlo[:, j, :]),
                            j == 0, j == K - 1)
            ins.then_inc(d0w_done, 1)
            pe.wait_ge(c0_sum, 2)
            turn_units(3, units_a0)

            def small0(t, half, xT):
                pe.wait_ge(xT_lo, t * 2 + 2)
                for k in range(K):
                    ins = three(p0[:, 0:C0C], (tile_of(xT[0], k, half), tile_of(xT[1], k, half)), (C0hi[:, k, :], C0lo[:, k, :]),
                                k == 0, k == K - 1, skip_group_check=True)
                ins.then_inc(p0_done, 1)

            def turn_small(s, nth, dst, src, done):
                pe.wait_ge(s, nth)
                pe.transpose(dst, src, ident[:, :]).then_inc(done, 1)

            def add_lora0(t):
                pe.wait_ge(hgT_lo, t + 1)
                three(p0[:, ER + E:C0C], (hgThi[:, :], hgTlo[:, :]), (D0hi[:, :], D0lo[:, :]), False, True,
                      skip_group_check=True).then_inc(z0_done, 1)

            def ffn0(q, g, bank):
                for n in range(2):
                    ins = three(bank[:, n * 2 * P:(n + 1) * 2 * P], split_of(BwThi, BwTlo, 2 * g + n),
                                (whThi[:, :], whTlo[:, :]), n == 0, n == 1, skip_group_check=True)
                ins.then_inc(x1w_done, 1)

            def fe_steps(s0, s1):
                for step in range(s0, s1):
                    c, k = step // K, step % K
                    c0, n = CHUNKS[c]
                    ins = three(m_psum(0, c), split_of(ws_hi[1], ws_lo[1], k),
                                (WbThi[:, k, c0:c0 + n], WbTlo[:, k, c0:c0 + n]), k == 0, k == K - 1)
                    if k == K - 1:
                        ins.then_inc(fe_done, 1)

            turn_units(NU1, units_second[:NEF - NU1])
            pe.wait_ge(c0_lo, 2)
            pe.wait_ge(d0w_lo, 1)
            small0(0, 0, xT_first)
            pe.wait_ge(brow_in, 16)
            pe.transpose(pt[:, 0:K], brow[:, :], ident[0:K, 0:K]).then_inc(bcol_turned, 1)
            pe.wait_ge(unit_lo, NEF)
            for n, unit in enumerate(units_second[NEF - NU1:NEF - NU1 + 10]):
                if n == 4:
                    turn_small(hg_ready, 1, pt_hg, hg[:, :], thg_done)
                if n == 8:
                    add_lora0(0)
                turn_units(NEF + n, [unit])
                if n == 8:
                    pe.wait_ge(unit_lo, wb_turned(5))
                fe_steps(n, n + 1)
            pe.wait_ge(fe_lo, 1)
            turn_x(xin_first[:, D:2 * D], XT_FIRST[1])
            turn_small(wh_ready, 1, pt_wh, wh[:, :], twh_done)
            turn_units(NEF + 10, units_bw)
            fe_steps(10, 12)
            small0(1, 1, xT_first)
            fe_steps(12, 2 * K)
            pe.wait_ge(unit_lo, NU2)
            fe_steps(2 * K, 18)
            turn_small(hg_ready, 2, pt_hg, hg[:, :], thg_done)
            fe_steps(18, 21)
            add_lora0(1)
            fe_steps(21, 3 * K)

            def m_chunk(i, par, c):
                c0, n = CHUNKS[c]
                for k in range(K):
                    ins = three(m_psum(M_BANKS[par], c), split_of(ws_hi[par], ws_lo[par], k),
                                (WbThi[:, k, c0:c0 + n], WbTlo[:, k, c0:c0 + n]), k == 0, k == K - 1)
                ins.then_inc(m_done, 1)

            for par in range(2):
                pe.wait_ge(w1_lo, par + 1)
                for c in range(3):
                    if par == 0:
                        pe.wait_ge(fe_lo, c + 1)
                    elif c < 2:
                        pe.wait_ge(x1_half, 1 + c)
                    m_chunk(0, par, c)
                    if par == 0 and c == 0:
                        turn_small(wh_ready, 2, pt_wh, wh[:, :], twh_done)
                    if par == 0 and c == 1:
                        pe.wait_ge(whT_lo, 2)
                        for g in range(4):
                            ffn0(0, g, X1W_FIRST[g])
            with pe.Fori(1, K // 2 - 1) as i:
                for par in range(2):
                    pe.wait_ge(w1_lo, i * 2 + par + 1)
                    for c in range(3):
                        pe.wait_ge(m_lo, i * 6 + par * 3 + c - 5)
                        m_chunk(i, par, c)
            pe.wait_ge(w1_lo, K - 1)
            for c in range(3):
                pe.wait_ge(m_lo, 3 * (K - 3) + c + 1 - 3)
                m_chunk(K // 2 - 1, 0, c)
            turn_units(NU2, units_b1)
            pe.wait_ge(w1_lo, K)
            pe.wait_ge(m_lo, 3 * (K - 2))
            m_chunk(K // 2 - 1, 1, 0)
            pe.wait_ge(x2_in, 16)
            pe.wait_ge(unit_lo, NU2 + 2)
            turn_x(x2_early, XT_EARLY)
            pe.wait_ge(acc_step, 1 + 2 * K)
            pe.wait_ge(gp_step, 3)
            pe.wait_ge(m_lo, 3 * (K - 1))
            for c, (c0, n) in enumerate(CHUNKS):
                pe.matmul(m_psum(0, c), ones[:, :], b_acc[:, c0:c0 + n], start=True, stop=True).then_inc(bias_done, 1)
            m_chunk(K // 2 - 1, 1, 1)
            m_chunk(K // 2 - 1, 1, 2)
            pe.wait_ge(brow_lo, 3)

            pe.wait_ge(m_lo, 3 * K - 1)
            pe.wait_ge(bias_step, 3)

            def turn_x_main(t, half, nth, waits):
                pe.wait_ge(x_in[half], nth * 16)
                for h in range(2):
                    if waits:
                        pe.wait_ge(*waits[h])
                    for k in range(4):
                        ins = pe.transpose(rows(XT_BANKS[half][h], k), rows(xin[half], 4 * h + k), ident[:, :])
                    ins.then_inc(tx_done, 1)

            def slot(b, turn, has_a, has_n, first=False):
                m, a, n, q = b * 2, b * 2 + 2, b * 2 + 4, b + 1
                xa = x1T[turn]
                late = 3 if first else 0
                done = [0]

                def main_to(until):
                    for step in range(done[0], min(until + late, 6 * K)):
                        half, c, k = step // (3 * K), step // K % 3, step % K
                        s = slice(c * PART, (c + 1) * PART)
                        if k == 0 and not (first and half == 0):
                            pe.wait_ge(y_ready, (m + half) * 3 - 2 + c)
                        if first and step < K and k % 2 == 0:
                            pe.wait_ge(x1T_lo, k // 2 + 1)
                        if first and step == 2 * K:
                            pe.wait_ge(m_lo, 3 * K)
                        ins = three(pm[c][:, 0:PART], (tile_of(xa[0], k, half), tile_of(xa[1], k, half)),
                                    (Mhi[:, k, s], Mlo[:, k, s]), k == 0, c == 0 and k == K - 1,
                                    skip_group_check=True)
                        if c == 0 and k == K - 1:
                            ins.then_inc(h1_done, 1)
                        done[0] = step + 1

                def lora(t, c):
                    y0, w = Y_OF[c]
                    y, s = pm[c][:, PART - w:PART], slice(y0, y0 + w)
                    three(y, (wzThi[:, :], wzTlo[:, :]), (B1Thi[:, s], B1Tlo[:, s]), False, False,
                          skip_group_check=True)
                    pe.matmul(y, hsT[:, :], Fbuf[:, s], start=False, stop=True, skip_group_check=True)\
                      .then_inc(main_done, 1)

                def turn_hs(t):
                    pe.wait_ge(hs_ready, t + 1)
                    pe.transpose(pt_h1[0:96, :], hs[:, :].bitcast(F32), ident[:, :]).then_inc(ths_done, 1)

                def adapter(t):
                    pe.wait_ge(hsT_ready, t + 1)
                    pe.wait_ge(e_in, b * 48 + 48 + 32)
                    pe.matmul(pm[0][:, R:ZC], hsT[:, :], Ebuf[:, :], start=False, stop=True,
                              skip_group_check=True).then_inc(z1_done, 1)

                if not first:
                    if has_a:
                        small0(a, 0, xT_main)
                    pe.wait_ge(x1T_lo, b * 4 + 4)
                pe.wait_ge(as_lo, b + 1)
                if first:
                    main_to(0)
                    small0(a, 0, xT_main)
                main_to(7)
                if has_a:
                    turn_small(hg_ready, a + 1, pt_hg, hg[:, :], thg_done)
                main_to(9)
                if has_a:
                    add_lora0(a)
                main_to(10)
                turn_hs(m)
                main_to(12)
                adapter(m)
                if first:
                    turn_x_main(a + 1, 1, 1, None)
                main_to(14)
                if has_a:
                    turn_small(wh_ready, a + 1, pt_wh, wh[:, :], twh_done)
                main_to(15)
                if has_a:
                    small0(a + 1, 1, xT_main)
                main_to(17)
                if has_a:
                    pe.wait_ge(whT_lo, a + 1)
                turn_small(wz_ready, m + 1, pt_wz, wz[:, :], twz_done)
                main_to(20)
                pe.wait_ge(wzT_lo, m + 1)
                pe.wait_ge(f_in, b * 48 + 48 + 32)
                lora(m, 0)
                lora(m, 1)
                main_to(22)
                if has_a:
                    turn_small(hg_ready, a + 2, pt_hg, hg[:, :], thg_done)
                main_to(24)
                lora(m, 2)
                if has_a:
                    add_lora0(a + 1)
                main_to(29)
                if has_a:
                    turn_small(wh_ready, a + 2, pt_wh, wh[:, :], twh_done)
                main_to(31)
                if has_a:
                    pe.wait_ge(whT_lo, a + 2)
                    for g in range(3):
                        ffn0(q, g, X1W_BANKS[g])
                main_to(34)
                turn_hs(m + 1)
                if has_a:
                    pe.wait_ge(x1_half, q * 4 + 1)
                    ffn0(q, 3, X1W_BANKS[3])
                main_to(35)
                adapter(m + 1)
                main_to(40)
                if has_n:
                    turn_x_main(n, 0, b + 1, [(x1_half, q * 4 + 2), (x1_half, q * 4 + 3)])
                main_to(44 if has_n else 46)
                turn_small(wz_ready, m + 2, pt_wz, wz[:, :], twz_done)
                main_to(47 if has_n else 48)
                pe.wait_ge(wzT_lo, m + 2)
                lora(m + 1, 0)
                lora(m + 1, 1)
                if has_n:
                    turn_x_main(n + 1, 1, b + 2, [(x1_half, q * 4 + 4), (xT_lo, n * 2 + 1)])
                main_to(48)
                lora(m + 1, 2)

            slot(0, 0, True, True, first=True)
            with pe.Fori(0, 2) as i:
                for turn in (1, 0):
                    slot(i * 2 + 2 - turn, turn, True, True)
            slot(NB - 3, 1, True, True)
            slot(NB - 2, 0, True, False)
            slot(NB - 1, 1, False, False)


_INS = ['x', 'itok_B_0_7', 'itok_B_0_23', 'L0_cond_W', 'L0_cond_Wr', 'L0_cond_A', 'L0_cond_B', 'L0_ffn_route_w',
        'L0_ffn_A', 'L0_ffn_Bw', 'L1_cond_W', 'L1_cond_b', 'L1_cond_lora_As', 'L1_cond_lora_Bs', 'L1_ffn_W_base',
        'L1_ffn_b_base', 'L1_ffn_W_router', 'L1_ffn_A', 'L1_ffn_B']


def kernel(**inputs):
    import numpy as _np
    import concourse.bacc as _bacc
    from concourse import mybir as _mybir
    from concourse.bass_utils import run_bass_kernel_spmd as _run

    nc = _bacc.Bacc("TRN2", target_bir_lowering=False, num_devices=1)
    arrays, args = {}, []
    for name in _INS:
        a = _np.ascontiguousarray(inputs[name])
        arrays[f"in_{name}_dram"] = a
        args.append(nc.dram_tensor(f"in_{name}_dram", a.shape, _mybir.dt.from_np(a.dtype), kind="ExternalInput").ap())
    out = nc.dram_tensor("out_dram", inputs["x"].shape, F32, kind="ExternalOutput").ap()
    adaln_ffn(nc, *args, out)
    r = _run(nc, [arrays], core_ids=[0])
    return r.results[0]["out_dram"]
```
